# Optimizing a Trainium2 kernel written in Bass

```python
import numpy as np
import jax
import jax.numpy as jnp

def _softmax(x, axis=-1):
    return jax.nn.softmax(x, axis=axis)

def _gelu(x):
    return jax.nn.gelu(x, approximate=True)

def _silu(x):
    return jax.nn.silu(x)

def _sigmoid(x):
    return jax.nn.sigmoid(x)

def _layernorm(x, axis=-1, eps=1e-05):
    m = jnp.mean(x, axis=axis, keepdims=True)
    v = jnp.var(x, axis=axis, keepdims=True)
    return (x - m) / jnp.sqrt(v + eps)

def _scatter_add(tgt, idx, src, axis=0):
    return tgt.at[idx].add(src)

def _segment_sum(src, seg, n):
    return jax.ops.segment_sum(src, seg, n)
kernel_name = 'mk_adj_preln_d1_adj_r2_9347f2'

def setup_inputs(seed: int=0):
    np.random.seed(seed)
    _w = jnp.asarray

    def _rec_inputs():
        import jax
        import jax.numpy as jnp
        _gk = jax.random.key(seed)
        x = 7.22e-05 + 1 * jax.random.normal(jax.random.fold_in(_gk, 1), (32, 256, 512), jnp.float32)
        _a = jax.random.bernoulli(jax.random.fold_in(_gk, 2), 0.0078125, (32, 256, 256))
        _a = jnp.logical_or(_a, jnp.swapaxes(_a, -1, -2))
        _a = jnp.logical_or(_a, jnp.eye(256, dtype=bool))
        _af = _a.astype(jnp.float32)
        _af = _af * jax.random.uniform(jax.random.fold_in(_gk, 3), (32, 256, 256), jnp.float32, 0.05, 4.42607)
        adj = _af
        return (x, adj)
    x, adj = _rec_inputs()

    def _L0_gnn_setup():
        import jax, jax.numpy as jnp
        import numpy as np
        NUM_HEADS = 16
        key = jax.random.key(seed)
        ks = jax.random.split(key, 7)
        B, N, D = (16, 256, 512)
        return {'x': jax.random.normal(ks[0], (B, N, D), dtype=jnp.float32), 'spatial_encoding': jax.random.normal(ks[1], (B, N, N), dtype=jnp.float32), 'edge_encoding': jax.random.normal(ks[2], (B, N, N), dtype=jnp.float32), 'Wq': jax.random.normal(ks[3], (D, D), dtype=jnp.float32) * D ** (-0.5), 'Wk': jax.random.normal(ks[4], (D, D), dtype=jnp.float32) * D ** (-0.5), 'Wv': jax.random.normal(ks[5], (D, D), dtype=jnp.float32) * D ** (-0.5), 'Wo': jax.random.normal(ks[6], (D, D), dtype=jnp.float32) * D ** (-0.5)}
    _L0_gnn_all = _L0_gnn_setup()
    _L0_gnn_in = {k: v for k, v in _L0_gnn_all.items() if k in ('Wq', 'Wk', 'Wv', 'Wo')}
    del _L0_gnn_all
    return {'x': x, 'adj': adj, 'L0_gnn_Wq': _L0_gnn_in['Wq'], 'L0_gnn_Wk': _L0_gnn_in['Wk'], 'L0_gnn_Wv': _L0_gnn_in['Wv'], 'L0_gnn_Wo': _L0_gnn_in['Wo']}

def reference(x, adj, L0_gnn_Wq, L0_gnn_Wk, L0_gnn_Wv, L0_gnn_Wo):
    import jax
    import jax.numpy as jnp

    def _L0_gnn_ref(x, spatial_encoding, edge_encoding, Wq, Wk, Wv, Wo):
        import jax, jax.numpy as jnp
        import numpy as np
        NUM_HEADS = 16
        B, N, D = x.shape
        H = NUM_HEADS
        hd = D // H
        scale = D ** (-0.5)

        def split_heads(t):
            return t.reshape(B, N, H, hd).transpose(0, 2, 1, 3)
        q = split_heads(x @ Wq.T)
        k = split_heads(x @ Wk.T)
        v = split_heads(x @ Wv.T)
        bias = (spatial_encoding + edge_encoding)[:, None]
        a = jnp.einsum('bhnd,bhmd->bhnm', q, k) * scale + bias
        row_nonzero = jnp.any(a != 0, axis=-1, keepdims=True)
        a = jnp.where(row_nonzero, a, -jnp.inf)
        p = jax.nn.softmax(a, axis=-1)
        p = jnp.where(jnp.isnan(p), 0.0, p)
        o = jnp.einsum('bhnm,bhmd->bhnd', p, v)
        o = o.transpose(0, 2, 1, 3).reshape(B, N, D)
        return o @ Wo.T
    h = jnp.maximum(_layernorm(x, axis=-1), 0.0)
    x = x + _L0_gnn_ref(h, adj, adj, L0_gnn_Wq, L0_gnn_Wk, L0_gnn_Wv, L0_gnn_Wo)
    return x

_drawn_inputs = setup_inputs


def setup_inputs(seed=0):
    import zlib

    import numpy as np

    out = dict(_drawn_inputs(seed))
    spreads = {}
    factors = {'L0_gnn_Wq': 3.433, 'L0_gnn_Wk': 3.386}
    for name, (base, spread) in spreads.items():
        noise = np.random.default_rng([zlib.crc32(name.encode()), seed]).standard_normal(out[name].shape)
        drawn = base * np.exp(spread * noise) if base else spread * noise
        out[name] = jnp.asarray(drawn.astype(out[name].dtype))
    for name, factor in factors.items():
        out[name] = (out[name] * factor).astype(out[name].dtype)
    return out
```

```python
import numpy as np
import concourse.bass as bass
from concourse import mybir
from contextlib import ExitStack

F32 = mybir.dt.float32
F16 = mybir.dt.float16
I32 = mybir.dt.int32
ACT = mybir.ActivationFunctionType
ALU = mybir.AluOpType
AX = mybir.AxisListType

NB, N, D, H = 32, 256, 512, 16
HD = D // H
P = 128
NU = N // P
NC = D // P
HC = P // HD
NK = 3

EPS = 1e-5
H_UP = 10
W_UP = 14
DOWN = 2.0 ** -19
UP = H_UP + W_UP - 19
K_UP = 16.0 * D ** -0.5
K_SUM_DOWN = 1.0 / N

JOBS = ("q01", "q23", "k01", "k23", "o0", "o1", "v0", "v1")
NJ = len(JOBS)


class Slot:

    def __init__(self, i, off, prev, cur, nxt):
        self.i, self.off = i, off
        self.prev, self.cur, self.nxt = prev, cur, nxt
        self.first = i == 0 and off == -1 if isinstance(i, int) else False

    def batch(self, d):
        return 2 * self.i + (self.off + d)

    def par(self, d):
        return (self.off + d) % 2

    def half(self, d):
        return self.i + (self.off + d) // 2

    def has(self, d):
        return {-1: self.prev, 0: self.cur, 1: self.nxt}[d]

    def uses(self, j):
        return self.prev if j in (4, 5) else self.nxt


def emit(nc, x_d, adj_d, wq_d, wk_d, wv_d, wo_d, out_d):
    xv = x_d.rearrange("b (u p) d -> b p u d", p=P)
    av = adj_d.rearrange("b (u p) m -> b p u m", p=P)
    ov = out_d.rearrange("b (u p) d -> b p u d", p=P)

    ctx = ExitStack()
    with ctx:
        def sb(name, shape, dt=F32):
            return ctx.enter_context(nc.sbuf_tensor(name, shape, dt))

        def sem(name):
            return ctx.enter_context(nc.semaphore(name))

        ident = sb("ident", [P, P])
        head_mask = sb("head_mask", [P, HC])
        w_nat = sb("w_nat", [P, 4, NC, D])
        w_hi = sb("w_hi", [P, 4, NC, D], F16)
        w_lo = sb("w_lo", [P, 4, NC, D], F16)
        w_max = sb("w_max", [P, 4])
        w_row_max = sb("w_row_max", [1, 4])
        ones_row = sb("ones_row", [1, P])
        w_top = sb("w_top", [P, 4])
        w_pow = sb("w_pow", [P, 4])
        w_inv = sb("w_inv", [P, 4])
        w_up = sb("w_up", [P, 4])
        w_scale = sb("w_scale", [P, 4])
        sigma = sb("sigma", [P, 1])
        adj_scale = sb("adj_scale", [P, 1])
        out_scale = sb("out_scale", [P, 1])
        xs = sb("xs", [P, 2, NU, D])
        xn = sb("xn", [P, NU, D])
        x_res = sb("x_res", [P, 2, NU, D])
        adj_raw = sb("adj_raw", [P, 2, NU, N])
        adj_s = sb("adj_s", [P, 2, NU, N])
        adj_max = sb("adj_max", [P, 2, NU])
        stats = sb("stats", [P, NU, 6])
        mean_var = sb("mean_var", [P, NU, 2])
        neg_mean = sb("neg_mean", [P, NU])
        var_s = sb("var_s", [P, NU])
        rstd = sb("rstd", [P, NU])
        minus_half = sb("minus_half", [P, NU])
        ht_hi = sb("ht_hi", [P, 2, NC, N], F16)
        ht_lo = sb("ht_lo", [P, 2, NC, N], F16)
        q_hi = sb("q_hi", [P, NC, N], F16)
        q_lo = sb("q_lo", [P, NC, N], F16)
        k_hi = sb("k_hi", [P, NC, N], F16)
        k_lo = sb("k_lo", [P, NC, N], F16)
        k_sum = sb("k_sum", [P, NC])
        k_diag = sb("k_diag", [P, NC, HC], F16)
        q_stack = sb("q_stack", [NK * HD, 2, HC, NC, N], F16)
        k_stack = sb("k_stack", [NK * HD, 2, HC, NC, N], F16)
        v_sb = sb("v_sb", [P, 2, NU, D])
        logits = sb("logits", [P, 4, NU, N])
        probs = sb("probs", [P, 4, NU, N])
        row_min = sb("row_min", [P, 2, NU, H])
        row_sum = sb("row_sum", [P, 2, NU, H])
        some_qk = sb("some_qk", [P, 2, NU, H])
        some = sb("some", [P, NU, HC])
        recip = sb("recip", [P, NU, HC])
        recip_kept = sb("recip_kept", [P, NU, HC])
        recip_wide = sb("recip_wide", [P, NU, HC, HD])
        recip_t = sb("recip_t", [P, N])
        probs_t = sb("probs_t", [P, 8, NU, N])
        o_norm = sb("o_norm", [P, 2, N])
        o_hi = sb("o_hi", [P, 2, NC, N], F16)
        o_lo = sb("o_lo", [P, 2, NC, N], F16)

        ps = ctx.enter_context(nc.psum_tensor("ps", [P, 8, 512], F32))
        S_BANK, PT_BANK, PV_BANK, PJ_BANK, AUX_BANK = 0, 2, 4, 5, 7
        W_BANKS, TOP_BANK, ROW_BANK = 5, 5, 6

        waits_met = sem("waits_met")
        w_in = [sem(f"w_in{w}") for w in range(4)]
        x_in = [sem(f"x_in{i}") for i in range(2)]
        adj_in = [sem(f"adj_in{i}") for i in range(2)]
        xres_in = [sem(f"xres_in{i}") for i in range(2)]
        out_done = [sem(f"out_done{i}") for i in range(2)]
        q_stacked = sem("q_stacked")
        k_stacked = [sem("k_stacked01"), sem("k_stacked23")]
        consts_set = sem("consts_set")
        ident_set = sem("ident_set")
        consts_dve = sem("consts_dve")
        w_max_found = sem("w_max_found")
        ones_set = sem("ones_set")
        w_row_turned = sem("w_row_turned")
        w_row_max_found = sem("w_row_max_found")
        w_top_found = sem("w_top_found")
        scale_step = sem("scale_step")
        scales_ready = sem("scales_ready")
        wt_ready = sem("wt_ready")
        wt_hi_taken = sem("wt_hi_taken")
        wt_taken = sem("wt_taken")
        stat_step = sem("stat_step")
        ln_stats = sem("ln_stats")
        rstd_ready = sem("rstd_ready")
        xn_ready = sem("xn_ready")
        adj_scaled = sem("adj_scaled")
        adj_checked = sem("adj_checked")
        aux_full = sem("aux_full")
        aux_hi = sem("aux_hi")
        aux_taken = sem("aux_taken")
        pj_full = sem("pj_full")
        pj_hi = sem("pj_hi")
        pj_taken = [sem(f"pj_taken{i}") for i in range(2)]
        k_diag_ready = sem("k_diag_ready")
        scores_ready = sem("scores_ready")
        logits_ready = sem("logits_ready")
        probs_ready = sem("probs_ready")
        pt_full = sem("pt_full")
        pt_taken = [sem(f"pt_taken{i}") for i in range(2)]
        pv_done = sem("pv_done")
        recip_step = sem("recip_step")
        recip_ready = sem("recip_ready")
        recip_spread = sem("recip_spread")
        rt_full = sem("rt_full")
        rt_taken = sem("rt_taken")
        o_norm_ready = sem("o_norm_ready")
        o_hi_ready = sem("o_hi_ready")
        o_split = sem("o_split")

        def need(eng, s, value):
            if isinstance(value, int) and value <= 0:
                return
            eng.wait_ge(s, value)

        def settle(eng):
            eng.sem_inc(waits_met, 1)

        def pj_full_at(t, j):
            return NJ * t.batch(1) + (j + 1)

        def pj_taken_at(t, j):
            return (NJ // 2) * t.batch(1) + (j // 2 + 1)

        def full_step(t, j):
            if t.nxt:
                return 3 if j == 3 and not t.prev else 1
            return {4: 5, 5: 3}[j]

        def taken_step(t, j):
            if t.nxt:
                return 2 if j in (2, 3) and not t.prev else 1
            return 4

        def bank_free_at(t, j):
            return pj_taken_at(t, j) - (1 if t.nxt else 3)

        def aux_at(t, k):
            return 3 * t.batch(1) + (k + 3)

        def head(t, s):
            d = s // H
            return (d, s % H) if t.has(d) else (None, None)

        first = Slot(0, -1, False, False, True)
        second = Slot(0, 0, False, True, True)

        def pair(i):
            a = Slot(i, 1, True, True, True)
            return a, Slot(i, 2, True, True, True)

        last = Slot(0, NB - 1, True, True, False)
        tail = Slot(0, NB, True, False, False)
        LOOPS = (NB - 2) // 2

        def run(eng, slot):
            slot(first)
            slot(second)
            with eng.Fori(0, LOOPS) as i:
                for t in pair(i):
                    slot(t)
            slot(last)
            slot(tail)

        block = ctx.enter_context(nc.Block())

        @block.sync
        def _(sp):
            sp.dma_start(xs[:, 0], xv[0]).then_inc(x_in[0], 16)
            for w, w_d in ((0, wq_d), (1, wk_d), (2, wv_d)):
                sp.dma_start(w_nat[:, w], w_d.rearrange("(o p) k -> p o k", p=P)).then_inc(w_in[w], 16)
            sp.dma_start(xs[:, 1], xv[1]).then_inc(x_in[1], 16)
            sp.dma_start(adj_raw[:, 0], av[0]).then_inc(adj_in[0], 16)
            sp.dma_start(w_nat[:, 3], wo_d.rearrange("(o p) k -> p o k", p=P)).then_inc(w_in[3], 16)
            for i in range(2):
                sp.sem_inc(out_done[i], 16 * NU)

            def stack(t, dst, parts, chunks, signal):
                c0, c1 = chunks
                for blk, part in enumerate(parts):
                    for j in range(HC):
                        sp.dma_start(dst[HD * blk:HD * blk + HD, t.par(1), j, c0:c1, :],
                                     part[HD * j:HD * j + HD, c0:c1, :]).then_inc(signal, 16)

            def slot(t):
                if t.nxt:
                    sp.wait_ge(xn_ready, NU * t.batch(2))
                    sp.dma_start(xs[:, t.par(3)], xv[wrap(t, 3)]).then_inc(x_in[t.par(3)], 16)
                    need(sp, adj_scaled, t.batch(1))
                    need(sp, adj_checked, t.batch(1))
                    sp.dma_start(adj_raw[:, t.par(2)], av[wrap(t, 2)]).then_inc(adj_in[t.par(2)], 16)
                if t.cur:
                    sp.wait_ge(out_done[t.par(0)], 16 * NU * t.half(0) + 16 * NU)
                    sp.dma_start(x_res[:, t.par(0)], xv[t.batch(0)]).then_inc(xres_in[t.par(0)], 16)
                if t.nxt:
                    need(sp, scores_ready, H * t.batch(0))
                    sp.wait_ge(pj_taken[0], pj_taken_at(t, 0))
                    sp.wait_ge(pj_taken[1], pj_taken_at(t, 1))
                    stack(t, q_stack, (q_hi, q_hi, q_lo), (0, NC), q_stacked)
                    for g in range(2):
                        sp.wait_ge(pj_taken[g], pj_taken_at(t, 2 + g))
                        stack(t, k_stack, (k_hi, k_lo, k_hi), (2 * g, 2 * g + 2), k_stacked[g])
                if t.prev:
                    for u in range(NU):
                        sp.wait_ge(pj_taken[u], pj_taken_at(t, 4 + u))
                        sp.dma_start(ov[t.batch(-1)][:, u, :], x_res[:, t.par(-1), u, :])\
                          .then_inc(out_done[t.par(-1)], 16)

            def wrap(t, d):
                b = t.batch(d)
                return b % NB

            run(sp, slot)
            for i in range(2):
                sp.wait_ge(out_done[i], 16 * NU * (NB // 2 + 1))
                sp.wait_ge(x_in[i], 16 * (NB // 2 + 1))
                sp.wait_ge(adj_in[i], 16 * (NB // 2 + (i == 0)))

        @block.gpsimd
        def _(pool):
            g = nc.gpsimd
            g.memset(ident[:], 0.0).then_inc(consts_set, 1)
            g.memset(minus_half[:], -0.5).then_inc(consts_set, 1)
            pool.wait_ge(consts_set, 2)
            g.affine_select(out=ident[:], in_=ident[:], compare_op=ALU.not_equal, fill=1.0, base=0,
                            pattern=[[-1, P]], channel_multiplier=1).then_inc(ident_set, 1)
            pool.wait_ge(ident_set, 1)
            g.memset(ones_row[:], 1.0).then_inc(ones_set, 1)

            def layernorm(t, d):
                pool.wait_ge(ln_stats, NU * (t.batch(d) + 1))
                g.tensor_tensor(rstd[:], var_s[:], minus_half[:], ALU.pow).then_inc(rstd_ready, 1)
                pool.wait_ge(rstd_ready, t.batch(d) + 1)
                if d == 2:
                    pool.wait_ge(aux_full, aux_at(t, 1) - 3 if not t.first else 2)
                settle(pool)
                for u in range(NU):
                    g.tensor_scalar(xn[:, u, :], xs[:, t.par(d), u, :], neg_mean[:, u:u + 1],
                                    rstd[:, u:u + 1], ALU.add, ALU.mult).then_inc(xn_ready, 1)

            layernorm(first, 1)

            def scale_adj(t):
                pool.wait_ge(adj_in[t.par(1)], 16 * t.half(1) + 16)
                need(pool, logits_ready, NU * H * t.batch(0))
                settle(pool)
                g.tensor_scalar(adj_s[:, t.par(1)], adj_raw[:, t.par(1)], adj_scale[:, 0:1], 1.0,
                                ALU.mult, ALU.mult).then_inc(adj_scaled, 1)

            def spread(t, d, c):
                pool.wait_ge(recip_ready, NC * t.batch(d) + (c + 1))
                need(pool, rt_full, NC * t.batch(d) + c)
                settle(pool)
                g.tensor_copy(recip_wide[:], recip_kept[:].unsqueeze(3).broadcast_to([P, NU, HC, HD]))\
                 .then_inc(recip_spread, 1)

            def split_o(t, d, c):
                pool.wait_ge(o_norm_ready, NC * t.batch(d) + (c + 1))
                if c == 0:
                    pool.wait_ge(pj_full, NJ * t.batch(d) + 6)
                settle(pool)
                g.tensor_copy(o_hi[:, t.par(d), c, :], o_norm[:, c % 2, :]).then_inc(o_hi_ready, 1)
                pool.wait_ge(o_hi_ready, NC * t.batch(d) + (c + 1))
                g.tensor_tensor(o_lo[:, t.par(d), c, :], o_norm[:, c % 2, :], o_hi[:, t.par(d), c, :],
                                ALU.subtract).then_inc(o_split, 1)

            def slot(t):
                if t.first:
                    pool.wait_ge(scales_ready, 2)
                for s in range(H):
                    if s == 0 and t.nxt:
                        scale_adj(t)
                    if s == 2:
                        if t.prev:
                            split_o(t, -1, NC - 1)
                        if t.nxt:
                            layernorm(t, 2)
                    if s == 9 and t.nxt:
                        pool.wait_ge(pj_hi, 4 * t.batch(1) + 4)
                        g.tensor_tensor(k_diag[:], k_sum[:].unsqueeze(2).broadcast_to([P, NC, HC]),
                                        head_mask[:].unsqueeze(1).broadcast_to([P, NC, HC]), ALU.mult)\
                         .then_inc(k_diag_ready, 1)
                    if s % 4 == 3 and t.cur:
                        spread(t, 0, s // 4)
                    if s % 4 == 2 and s >= 6 and t.cur:
                        split_o(t, 0, s // 4 - 1)

            run(pool, slot)

        @block.scalar
        def _(act):
            a = nc.scalar
            for w in range(4):
                act.wait_ge(scales_ready, w + 1)
                for kc in range(NC):
                    n = NC * w + kc
                    act.wait_ge(wt_ready, n + 1)
                    a.activation(w_hi[:, w, kc, :], ps[:, n % W_BANKS, :], ACT.Copy, scale=w_scale[:, w:w + 1])\
                     .then_inc(wt_hi_taken, 1)

            def take_h(t, d, k, full):
                act.wait_ge(aux_full, full)
                a.activation(ht_hi[:, t.par(d), 2 * k:2 * k + 2, :],
                             ps[:, AUX_BANK, :].rearrange("p (c n) -> p c n", c=2), ACT.Relu)\
                 .then_inc(aux_hi, 1)

            for k in range(2):
                take_h(first, 1, k, k + 1)

            def exp_rows(t, s):
                d, h = head(t, s)
                if d is None:
                    return
                need(act, pt_full, H * t.batch(d) + (h - 3))
                for u in range(NU):
                    act.wait_ge(logits_ready, NU * H * t.batch(d) + (NU * h + u + 1))
                    e = a.activation(probs[:, h % 4, u, :], logits[:, h % 4, u, :], ACT.Exp,
                                     bias=row_min[:, t.par(d), u, h:h + 1], scale=-1.0,
                                     accum_out=row_sum[:, t.par(d), u, h:h + 1])
                e.then_inc(probs_ready, 1)

            def take_probs_t(t, s):
                d, h = head(t, s)
                if d is None or h % 4 == 3:
                    return
                act.wait_ge(pt_full, H * t.batch(d) + (h + 1))
                need(act, pv_done, NC * t.batch(d) + (h // HC - 1))
                a.activation(probs_t[:, h % 8], ps[:, PT_BANK + h % 2, :].rearrange("p (m n) -> p m n", m=NU),
                             ACT.Copy).then_inc(pt_taken[h % 2], 1)

            def take_recip(t, d, c):
                act.wait_ge(rt_full, NC * t.batch(d) + (c + 1))
                need(act, o_norm_ready, NC * t.batch(d) + c)
                a.activation(recip_t[:], ps[:, PV_BANK, N:2 * N], ACT.Copy).then_inc(rt_taken, 1)

            def take_q(t, g):
                act.wait_ge(pj_full, pj_full_at(t, g))
                if g == 0:
                    need(act, q_stacked, 16 * NK * HC * t.batch(1))
                    if not t.first:
                        act.wait_ge(aux_full, aux_at(t, 2) - 3)
                a.activation(q_hi[:, 2 * g:2 * g + 2, :],
                             ps[:, PJ_BANK + g, :].rearrange("p (c n) -> p c n", c=2), ACT.Copy,
                             scale=-DOWN).then_inc(pj_hi, 1)

            def take_k(t, g):
                act.wait_ge(pj_full, pj_full_at(t, 2 + g))
                need(act, k_stacked[g], 16 * NK * HC * t.batch(1))
                for c in range(2):
                    e = a.activation(k_hi[:, 2 * g + c, :], ps[:, PJ_BANK + g, N * c:N * c + N], ACT.Copy,
                                     scale=DOWN, accum_out=k_sum[:, 2 * g + c:2 * g + c + 1])
                e.then_inc(pj_hi, 1)

            def take_v(t, d, u):
                act.wait_ge(pj_full, NJ * t.batch(d) + (7 + u))
                need(act, pv_done, NC * t.batch(d - 1))
                a.activation(v_sb[:, t.par(d), u, :], ps[:, PJ_BANK + u, :], ACT.Copy, scale=DOWN)\
                 .then_inc(pj_taken[u], 1)

            def slot(t):
                for s in range(H):
                    take_probs_t(t, s - 1)
                    if s == 0 and t.cur:
                        take_v(t, 0, 1)
                    if s == 2 and t.prev:
                        take_recip(t, -1, NC - 1)
                    if s % 4 == 2 and s >= 6 and t.cur:
                        take_recip(t, 0, s // 4 - 1)
                    if t.nxt:
                        if s in (2, 4):
                            take_q(t, s // 2 - 1)
                        if s in (6, 8):
                            take_k(t, s // 2 - 3)
                        if s in (7, 10):
                            take_h(t, 2, (s - 7) // 3, aux_at(t, (s - 7) // 3))
                        if s == 14:
                            take_v(t, 1, 0)
                    exp_rows(t, s + 1)

            run(act, slot)

        @block.vector
        def _(dve):
            v = nc.vector
            v.memset(w_up[:], 2.0 ** W_UP).then_inc(consts_dve, 1)
            v.memset(head_mask[:], 0.0).then_inc(consts_dve, 1)
            dve.wait_ge(consts_dve, 2)
            v.memset(w_up[:, 1:2], K_UP * 2.0 ** W_UP).then_inc(consts_dve, 1)
            for j in range(HC):
                v.memset(head_mask[HD * j:HD * j + HD, j:j + 1], K_SUM_DOWN).then_inc(consts_dve, 1)
            dve.wait_ge(consts_dve, 3 + HC)

            def ln_statistics(t, d):
                dve.wait_ge(x_in[t.par(d)], 16 * t.half(d) + 16)
                b = t.batch(d)
                for u in range(NU):
                    v.bn_stats(stats[:, u, :], xs[:, t.par(d), u, :]).then_inc(stat_step, 1)
                for u in range(NU):
                    dve.wait_ge(stat_step, 4 * b + (u + 1))
                    settle(dve)
                    v.bn_aggr(mean_var[:, u, :], stats[:, u, :]).then_inc(stat_step, 1)
                dve.wait_ge(stat_step, 4 * b + 4)
                v.tensor_scalar(neg_mean[:], mean_var[:, :, 0], -1.0, None, ALU.mult).then_inc(ln_stats, 1)
                v.tensor_scalar(var_s[:], mean_var[:, :, 1], EPS, 2.0 ** (-2 * H_UP), ALU.add, ALU.mult)\
                 .then_inc(ln_stats, 1)

            ln_statistics(first, 1)

            step = 0
            for w in range(4):
                one = slice(w, w + 1)
                dve.wait_ge(w_in[w], 16)
                v.tensor_reduce(out=w_max[:, one], in_=w_nat[:, w].rearrange("p o k -> p (o k)"),
                                axis=AX.X, op=ALU.max, apply_absolute_value=True).then_inc(w_max_found, 1)
                dve.wait_ge(w_row_turned, w + 1)
                v.reduce_max(w_row_max[0:1, one], ps[0:1, ROW_BANK, 0:P], AX.X).then_inc(w_row_max_found, 1)
                dve.wait_ge(w_top_found, w + 1)
                v.tensor_scalar(w_top[:, one], ps[:, TOP_BANK, one], 2.0 ** (-20 if w < 2 else -60), None, ALU.max)\
                 .then_inc(scale_step, 1)
                dve.wait_ge(scale_step, step + 1)
                v.tensor_scalar(w_pow[:, one].bitcast(I32), w_top[:, one].bitcast(I32), 0x7F800000, None,
                                ALU.bitwise_and).then_inc(scale_step, 1)
                dve.wait_ge(scale_step, step + 2)
                v.reciprocal(w_inv[:, one], w_pow[:, one]).then_inc(scale_step, 1)
                dve.wait_ge(scale_step, step + 3)
                step += 3
                if w == 1:
                    v.tensor_scalar(sigma[:], w_pow[:, 0:1], w_pow[:, 1:2], 2.0 ** -(2 * UP + 4),
                                    ALU.mult, ALU.mult)
                    v.tensor_scalar(adj_scale[:], w_inv[:, 0:1], w_inv[:, 1:2], -2.0 * 2.0 ** (2 * UP + 4),
                                    ALU.mult, ALU.mult)
                if w == 3:
                    v.tensor_scalar(out_scale[:], w_pow[:, 2:3], w_pow[:, 3:4], 2.0 ** -(UP + W_UP),
                                    ALU.mult, ALU.mult)
                v.tensor_tensor(w_scale[:, one], w_inv[:, one], w_up[:, one], ALU.mult)\
                 .then_inc(scales_ready, 1)
                dve.wait_ge(scales_ready, w + 1)
                for kc in range(NC):
                    n = NC * w + kc
                    dve.wait_ge(wt_hi_taken, n + 1)
                    v.scalar_tensor_tensor(out=w_lo[:, w, kc, :], in0=ps[:, n % W_BANKS, :],
                                           scalar=w_scale[:, w:w + 1], in1=w_hi[:, w, kc, :],
                                           op0=ALU.mult, op1=ALU.subtract).then_inc(wt_taken, 1)

            def take_h(t, d, k, n_hi):
                dve.wait_ge(aux_hi, n_hi)
                two = ps[:, AUX_BANK, :].rearrange("p (c n) -> p c n", c=2)
                v.scalar_tensor_tensor(out=ht_lo[:, t.par(d), 2 * k:2 * k + 2, :], in0=two, scalar=0.0,
                                       in1=ht_hi[:, t.par(d), 2 * k:2 * k + 2, :],
                                       op0=ALU.max, op1=ALU.subtract).then_inc(aux_taken, 1)

            for k in range(2):
                take_h(first, 1, k, k + 1)

            def logit_rows(t, s):
                d, h = head(t, s)
                if d is None:
                    return
                dve.wait_ge(scores_ready, H * t.batch(d) + (h + 1))
                if h == 0:
                    dve.wait_ge(adj_scaled, t.batch(d) + 1)
                need(dve, probs_ready, H * t.batch(d) + (h - 3))
                settle(dve)
                for u in range(NU):
                    v.tensor_tensor_reduce(out=logits[:, h % 4, u, :], in0=ps[:, S_BANK + h % 2, N * u:N * u + N],
                                           in1=adj_s[:, t.par(d), u, :], scale=sigma[:, 0:1], scalar=3e38,
                                           op0=ALU.add, op1=ALU.min,
                                           accum_out=row_min[:, t.par(d), u, h:h + 1]).then_inc(logits_ready, 1)

            def take_probs_t(t, s):
                d, h = head(t, s)
                if d is None or h % 4 != 3:
                    return
                dve.wait_ge(pt_full, H * t.batch(d) + (h + 1))
                need(dve, pv_done, NC * t.batch(d) + (h // HC - 1))
                v.tensor_copy(probs_t[:, h % 8], ps[:, PT_BANK + h % 2, :].rearrange("p (m n) -> p m n", m=NU))\
                 .then_inc(pt_taken[h % 2], 1)

            def invert(t, d, c):
                hs = slice(HC * c, HC * c + HC)
                n = 2 * NC * t.batch(d) + 2 * c
                dve.wait_ge(probs_ready, H * t.batch(d) + HC * (c + 1))
                v.reciprocal(recip[:], row_sum[:, t.par(d), :, hs]).then_inc(recip_step, 1)
                v.scalar_tensor_tensor(out=some[:], in0=row_min[:, t.par(d), :, hs], scalar=0.0,
                                       in1=some_qk[:, t.par(d), :, hs], op0=ALU.not_equal, op1=ALU.max)\
                 .then_inc(recip_step, 1)
                dve.wait_ge(recip_step, n + 2)
                need(dve, recip_spread, NC * t.batch(d) + c)
                v.scalar_tensor_tensor(out=recip_kept[:], in0=some[:], scalar=0.0, in1=recip[:],
                                       op0=ALU.not_equal, op1=ALU.mult).then_inc(recip_ready, 1)

            def normalize(t, d, c):
                dve.wait_ge(pv_done, NC * t.batch(d) + (c + 1))
                dve.wait_ge(rt_taken, NC * t.batch(d) + (c + 1))
                need(dve, o_split, NC * t.batch(d) + (c - 1))
                v.tensor_tensor(o_norm[:, c % 2, :], ps[:, PV_BANK, 0:N], recip_t[:], ALU.mult)\
                 .then_inc(o_norm_ready, 1)

            def take_qk(t, j):
                dve.wait_ge(pj_hi, 4 * t.batch(1) + (j + 1))
                g = j % 2
                hi, lo = (q_hi, q_lo) if j < 2 else (k_hi, k_lo)
                v.scalar_tensor_tensor(out=lo[:, 2 * g:2 * g + 2, :].rearrange("p c n -> p (c n)"),
                                       in0=ps[:, PJ_BANK + g, :], scalar=-DOWN if j < 2 else DOWN,
                                       in1=hi[:, 2 * g:2 * g + 2, :].rearrange("p c n -> p (c n)"),
                                       op0=ALU.mult, op1=ALU.subtract).then_inc(pj_taken[g], taken_step(t, j))

            def check_adj(t):
                dve.wait_ge(adj_in[t.par(1)], 16 * t.half(1) + 16)
                v.tensor_reduce(out=adj_max[:, t.par(1), :], in_=adj_raw[:, t.par(1)], axis=AX.X, op=ALU.max,
                                apply_absolute_value=True).then_inc(adj_checked, 1)

            def test_rows(t):
                dve.wait_ge(aux_full, aux_at(t, 2))
                dve.wait_ge(adj_checked, t.batch(1) + 1)
                v.scalar_tensor_tensor(out=some_qk[:, t.par(1)],
                                       in0=ps[:, AUX_BANK, 0:NU * H].rearrange("p (u h) -> p u h", u=NU),
                                       scalar=0.0,
                                       in1=adj_max[:, t.par(1), :].unsqueeze(2).broadcast_to([P, NU, H]),
                                       op0=ALU.not_equal, op1=ALU.max).then_inc(aux_taken, 1)

            def residual(t, u):
                dve.wait_ge(pj_full, pj_full_at(t, 4 + u))
                dve.wait_ge(xres_in[t.par(-1)], 16 * t.half(-1) + 16)
                v.scalar_tensor_tensor(out=x_res[:, t.par(-1), u, :], in0=ps[:, PJ_BANK + u, :],
                                       scalar=out_scale[:, 0:1], in1=x_res[:, t.par(-1), u, :],
                                       op0=ALU.mult, op1=ALU.add).then_inc(pj_taken[u], taken_step(t, 4 + u))

            def slot(t):
                for s in range(H):
                    logit_rows(t, s + 1)
                    take_probs_t(t, s - 1)
                    if s % 4 == 3 and t.cur:
                        invert(t, 0, s // 4)
                    if s == 2 and t.prev:
                        normalize(t, -1, NC - 1)
                    if s % 4 == 2 and s >= 6 and t.cur:
                        normalize(t, 0, s // 4 - 1)
                    if t.nxt:
                        if s == 1:
                            ln_statistics(t, 2)
                        if s in (2, 4, 6, 8):
                            take_qk(t, s // 2 - 1)
                        if s == 5:
                            check_adj(t)
                        if s in (7, 10):
                            k = (s - 7) // 3
                            take_h(t, 2, k, 2 * t.batch(2) + (k + 1))
                        if s == 14:
                            test_rows(t)
                    if t.prev and s in (10, 12):
                        residual(t, (s - 10) // 2)

            run(dve, slot)

        @block.tensor
        def _(pe):
            mm, tr = nc.tensor.matmul, nc.tensor.transpose
            pe.wait_ge(ident_set, 1)

            def turn_h(t, d, k, n):
                pe.wait_ge(xn_ready, NU * (t.batch(d) + 1))
                need(pe, aux_taken, n - 1)
                for c in range(2):
                    for u in range(NU):
                        m = tr(ps[:, AUX_BANK, N * c + P * u:N * c + P * u + P],
                               xn[:, u, P * (2 * k + c):P * (2 * k + c) + P], ident[:])
                m.then_inc(aux_full, 1)

            for w in range(4):
                pe.wait_ge(w_in[w], 16)
                for kc in range(NC):
                    n = NC * w + kc
                    need(pe, wt_taken, n - (W_BANKS - 1))
                    for o in range(NC):
                        m = tr(ps[:, n % W_BANKS, P * o:P * o + P], w_nat[:, w, o, P * kc:P * kc + P], ident[:])
                    m.then_inc(wt_ready, 1)
                pe.wait_ge(w_max_found, w + 1)
                tr(ps[0:1, ROW_BANK, 0:P], w_max[:, w:w + 1], ident[:]).then_inc(w_row_turned, 1)
                pe.wait_ge(ones_set, 1)
                pe.wait_ge(w_row_max_found, w + 1)
                need(pe, scales_ready, w)
                mm(ps[:, TOP_BANK, w:w + 1], ones_row[:], w_row_max[0:1, w:w + 1], start=True, stop=True)\
                    .then_inc(w_top_found, 1)
            pe.wait_ge(wt_taken, 4 * NC)
            for k in range(2):
                turn_h(first, 1, k, k + 1)

            THREE = ((0, 0), (0, 1), (1, 0))
            W = (w_hi, w_lo)
            HT = (ht_hi, ht_lo)
            O = (o_hi, o_lo)

            def part_products(t, j):
                out = []
                g = j % 2
                if j < 4:
                    w = j // 2
                    for c in range(2):
                        steps = [(kc, a, b) for kc in range(NC) for a, b in THREE]
                        for i, (kc, a, b) in enumerate(steps):
                            fs = P * (2 * g + c)
                            out.append((ps[:, PJ_BANK + g, N * c:N * c + N], W[a][:, w, kc, fs:fs + P],
                                        HT[b][:, t.par(1), kc, :], i == 0, i == len(steps) - 1))
                elif j < 6:
                    steps = [(c, a, b) for c in range(NC) for a, b in THREE]
                    for i, (c, a, b) in enumerate(steps):
                        out.append((ps[:, PJ_BANK + g, :], O[a][:, t.par(-1), c, P * g:P * g + P],
                                    W[b][:, 3, c, :], i == 0, i == len(steps) - 1))
                else:
                    steps = [(kc, a, b) for kc in range(NC) for a, b in THREE]
                    for i, (kc, a, b) in enumerate(steps):
                        out.append((ps[:, PJ_BANK + g, :], HT[a][:, t.par(1), kc, P * g:P * g + P],
                                    W[b][:, 2, kc, :], i == 0, i == len(steps) - 1))
                return out

            def project(t, s):
                j, part = s // 2, s % 2
                if not t.uses(j):
                    return
                if part == 0:
                    need(pe, pj_taken[j % 2], bank_free_at(t, j))
                    if j == 0:
                        pe.wait_ge(aux_taken, 2 if t.first else aux_at(t, 1) - 3)
                    if j == 4:
                        pe.wait_ge(o_split, NC * t.batch(0))
                products = part_products(t, j)
                half = len(products) // 2
                for o, l, r, start, stop in products[half * part:half * part + half]:
                    m = mm(o, l, r, start=start, stop=stop)
                if part == 1:
                    m.then_inc(pj_full, full_step(t, j))

            def scores(t, s):
                d, h = head(t, s)
                if d is None:
                    return
                c, j = h // HC, h % HC
                if h == 0:
                    pe.wait_ge(q_stacked, 16 * NK * HC * (t.batch(d) + 1))
                if h in (0, H // 2):
                    pe.wait_ge(k_stacked[h // (H // 2)], 16 * NK * HC * (t.batch(d) + 1))
                need(pe, logits_ready, NU * (H * t.batch(d) + (h - 1)))
                for u in range(NU):
                    m = mm(ps[:, S_BANK + h % 2, N * u:N * u + N], q_stack[:, t.par(d), j, c, P * u:P * u + P],
                           k_stack[:, t.par(d), j, c, :], start=True, stop=True)
                m.then_inc(scores_ready, 1)

            def turn_probs(t, s):
                d, h = head(t, s)
                if d is None:
                    return
                pe.wait_ge(probs_ready, H * t.batch(d) + (h + 1))
                need(pe, pt_taken[h % 2], (H // 2) * t.batch(d) + h // 2)
                for mh in range(NU):
                    for u in range(NU):
                        m = tr(ps[:, PT_BANK + h % 2, N * mh + P * u:N * mh + P * u + P],
                               probs[:, h % 4, u, P * mh:P * mh + P], ident[:])
                m.then_inc(pt_full, 1)

            def values(t, d, c):
                for i in range(2):
                    pe.wait_ge(pt_taken[i], (H // 2) * t.batch(d) + 2 * (c + 1))
                need(pe, o_norm_ready, NC * t.batch(d) + c)
                if c == 0:
                    for u in range(NU):
                        pe.wait_ge(pj_taken[u], (NJ // 2) * (t.batch(d) + 1))
                for mh in range(NU):
                    for j in range(HC):
                        h = HC * c + j
                        m = mm(ps[HD * j:HD * j + HD, PV_BANK, 0:N],
                               v_sb[:, t.par(d), mh, HD * h:HD * h + HD], probs_t[:, h % 8, mh, :],
                               start=(mh == 0), stop=(mh == NU - 1))
                m.then_inc(pv_done, 1)

            def turn_recip(t, d, c):
                pe.wait_ge(recip_spread, NC * t.batch(d) + (c + 1))
                for u in range(NU):
                    m = tr(ps[:, PV_BANK, N + P * u:N + P * u + P],
                           recip_wide[:, u].rearrange("p j f -> p (j f)"), ident[:])
                m.then_inc(rt_full, 1)

            def row_test(t):
                pe.wait_ge(k_diag_ready, t.batch(1) + 1)
                pe.wait_ge(aux_taken, aux_at(t, 2) - 1)
                for u in range(NU):
                    for c in range(NC):
                        m = mm(ps[:, AUX_BANK, H * u + HC * c:H * u + HC * c + HC],
                               q_hi[:, c, P * u:P * u + P], k_diag[:, c, :], start=True, stop=True)
                m.then_inc(aux_full, 1)

            def slot(t):
                for s in range(H):
                    scores(t, s + 2)
                    if s == 1 and t.prev:
                        turn_recip(t, -1, NC - 1)
                    if t.cur and s >= 4 and s % 4 == 1:
                        turn_recip(t, 0, s // 4 - 1)
                    project(t, s)
                    turn_probs(t, s)
                    if t.nxt:
                        if s in (6, 9):
                            turn_h(t, 2, (s - 6) // 3, aux_at(t, (s - 6) // 3))
                        if s == 13:
                            row_test(t)
                    if s == 0 and t.prev:
                        values(t, -1, NC - 1)
                    if t.cur and s >= 4 and s % 4 == 0:
                        values(t, 0, s // 4 - 1)

            run(pe, slot)


_INS = ["x", "adj", "L0_gnn_Wq", "L0_gnn_Wk", "L0_gnn_Wv", "L0_gnn_Wo"]


def kernel(**inputs):
    import numpy as _np
    import concourse.bacc as _bacc
    from concourse import mybir as _mybir
    from concourse.bass_utils import run_bass_kernel_spmd as _run

    nc = _bacc.Bacc("TRN2", target_bir_lowering=False, num_devices=1)
    arrays, args = {}, []
    for name in _INS:
        a = _np.ascontiguousarray(inputs[name])
        arrays[f"in_{name}"] = a
        args.append(nc.dram_tensor(f"in_{name}", a.shape, _mybir.dt.from_np(a.dtype), kind="ExternalInput").ap())
    out = nc.dram_tensor("out_0", inputs["x"].shape, _mybir.dt.float32, kind="ExternalOutput").ap()
    emit(nc, *args, out)
    return _run(nc, [arrays], core_ids=[0]).results[0]["out_0"]
```

```python
import concourse.bass as bass
from concourse import mybir
from contextlib import ExitStack

F32 = mybir.dt.float32
F16 = mybir.dt.float16
I32 = mybir.dt.int32
ACT = mybir.ActivationFunctionType
ALU = mybir.AluOpType
AX = mybir.AxisListType

NB, N, D, H = 32, 256, 512, 16
HD = D // H
P = 128
NU = N // P
NC = D // P
HC = P // HD
NK = 3

EPS = 1e-5
H_UP = 10
W_UP = 14
DOWN = 2.0 ** -19
UP = H_UP + W_UP - 19
K_UP = 16.0 * D ** -0.5
K_SUM_DOWN = 1.0 / N

JOBS = ("q01", "q23", "k01", "k23", "o0", "o1", "v0", "v1")
NJ = len(JOBS)


class Slot:

    def __init__(self, i, off, prev, cur, nxt):
        self.i, self.off = i, off
        self.prev, self.cur, self.nxt = prev, cur, nxt
        self.first = i == 0 and off == -1 if isinstance(i, int) else False

    def batch(self, d):
        return 2 * self.i + (self.off + d)

    def par(self, d):
        return (self.off + d) % 2

    def half(self, d):
        return self.i + (self.off + d) // 2

    def has(self, d):
        return {-1: self.prev, 0: self.cur, 1: self.nxt}[d]

    def uses(self, j):
        return self.prev if j in (4, 5) else self.nxt


def emit(nc, x_d, adj_d, wq_d, wk_d, wv_d, wo_d, out_d):
    xv = x_d.rearrange("b (u p) d -> b p u d", p=P)
    av = adj_d.rearrange("b (u p) m -> b p u m", p=P)
    ov = out_d.rearrange("b (u p) d -> b p u d", p=P)

    ctx = ExitStack()
    with ctx:
        def sb(name, shape, dt=F32):
            return ctx.enter_context(nc.sbuf_tensor(name, shape, dt))

        def sem(name):
            return ctx.enter_context(nc.semaphore(name))

        ident = sb("ident", [P, P])
        head_mask = sb("head_mask", [P, HC])
        w_nat = sb("w_nat", [P, 4, NC, D])
        w_hi = sb("w_hi", [P, 4, NC, D], F16)
        w_lo = sb("w_lo", [P, 4, NC, D], F16)
        w_max = sb("w_max", [P, 4])
        w_row_max = sb("w_row_max", [1, 4])
        ones_row = sb("ones_row", [1, P])
        w_top = sb("w_top", [P, 4])
        w_pow = sb("w_pow", [P, 4])
        w_inv = sb("w_inv", [P, 4])
        w_up = sb("w_up", [P, 4])
        w_scale = sb("w_scale", [P, 4])
        sigma = sb("sigma", [P, 1])
        adj_scale = sb("adj_scale", [P, 1])
        out_scale = sb("out_scale", [P, 1])
        xs = sb("xs", [P, 2, NU, D])
        xn = sb("xn", [P, NU, D])
        x_res = sb("x_res", [P, 2, NU, D])
        adj_raw = sb("adj_raw", [P, 2, NU, N])
        adj_s = sb("adj_s", [P, 2, NU, N])
        adj_max = sb("adj_max", [P, 2, NU])
        x_sum = sb("x_sum", [P, NU])
        stats = sb("stats", [P, NU, 6])
        mean_var = sb("mean_var", [P, NU, 2])
        neg_mean = sb("neg_mean", [P, NU])
        var_s = sb("var_s", [P, NU])
        rstd = sb("rstd", [P, NU])
        minus_half = sb("minus_half", [P, NU])
        ht_hi = sb("ht_hi", [P, 2, NC, N], F16)
        ht_lo = sb("ht_lo", [P, 2, NC, N], F16)
        q_hi = sb("q_hi", [P, NC, N], F16)
        q_lo = sb("q_lo", [P, NC, N], F16)
        k_hi = sb("k_hi", [P, NC, N], F16)
        k_lo = sb("k_lo", [P, NC, N], F16)
        k_sum = sb("k_sum", [P, NC])
        k_diag = sb("k_diag", [P, NC, HC], F16)
        q_stack = sb("q_stack", [NK * HD, 2, HC, NC, N], F16)
        k_stack = sb("k_stack", [NK * HD, 2, HC, NC, N], F16)
        v_sb = sb("v_sb", [P, 2, NU, D])
        logits = sb("logits", [P, 4, NU, N])
        probs = sb("probs", [P, 4, NU, N])
        row_min = sb("row_min", [P, 2, NU, H])
        row_sum = sb("row_sum", [P, 2, NU, H])
        some_qk = sb("some_qk", [P, 2, NU, H])
        some = sb("some", [P, NU, HC])
        recip = sb("recip", [P, NU, HC])
        recip_kept = sb("recip_kept", [P, NU, HC])
        recip_wide = sb("recip_wide", [P, NU, HC, HD])
        recip_t = sb("recip_t", [P, N])
        probs_t = sb("probs_t", [P, 8, NU, N])
        o_norm = sb("o_norm", [P, 2, N])
        o_hi = sb("o_hi", [P, 2, NC, N], F16)
        o_lo = sb("o_lo", [P, 2, NC, N], F16)

        ps = ctx.enter_context(nc.psum_tensor("ps", [P, 8, 512], F32))
        S_BANK, PT_BANK, PV_BANK, PJ_BANK, AUX_BANK = 0, 2, 4, 5, 7
        W_BANKS, MAX_BANK, TOP_COL = 4, 4, P

        waits_met = sem("waits_met")
        w_in = [sem(f"w_in{w}") for w in range(4)]
        x_in = [sem(f"x_in{i}") for i in range(2)]
        adj_in = [sem(f"adj_in{i}") for i in range(2)]
        xres_in = [sem(f"xres_in{i}") for i in range(2)]
        out_done = [sem(f"out_done{i}") for i in range(2)]
        q_stacked = sem("q_stacked")
        k_stacked = [sem(f"k_stacked{j}") for j in range(HC)]
        consts_set = sem("consts_set")
        ident_set = sem("ident_set")
        consts_dve = sem("consts_dve")
        w_max_found = sem("w_max_found")
        ones_set = sem("ones_set")
        w_row_turned = sem("w_row_turned")
        w_row_max_found = sem("w_row_max_found")
        w_top_found = sem("w_top_found")
        scale_step = sem("scale_step")
        scales_ready = sem("scales_ready")
        wt_ready = sem("wt_ready")
        wt_hi_taken = sem("wt_hi_taken")
        wt_taken = sem("wt_taken")
        stat_step = sem("stat_step")
        ln_stats = sem("ln_stats")
        rstd_ready = sem("rstd_ready")
        xn_ready = sem("xn_ready")
        adj_scaled = sem("adj_scaled")
        adj_checked = sem("adj_checked")
        aux_full = sem("aux_full")
        aux_hi = sem("aux_hi")
        aux_taken = sem("aux_taken")
        pj_full = sem("pj_full")
        pj_hi = sem("pj_hi")
        pj_taken = [sem(f"pj_taken{i}") for i in range(2)]
        k_diag_ready = sem("k_diag_ready")
        scores_ready = sem("scores_ready")
        logits_ready = sem("logits_ready")
        probs_ready = sem("probs_ready")
        pt_full = sem("pt_full")
        pt_taken = [sem(f"pt_taken{i}") for i in range(2)]
        pv_done = sem("pv_done")
        recip_step = sem("recip_step")
        recip_ready = sem("recip_ready")
        recip_spread = sem("recip_spread")
        rt_full = sem("rt_full")
        rt_taken = sem("rt_taken")
        o_norm_ready = sem("o_norm_ready")
        o_hi_ready = sem("o_hi_ready")
        o_split = sem("o_split")

        def need(eng, s, value):
            if isinstance(value, int) and value <= 0:
                return
            eng.wait_ge(s, value)

        def settle(eng):
            eng.sem_inc(waits_met, 1)

        def pj_full_at(t, j):
            return NJ * t.batch(1) + (j + 1)

        def pj_taken_at(t, j):
            return (NJ // 2) * t.batch(1) + (j // 2 + 1)

        def full_step(t, j):
            if t.nxt:
                return 3 if j == 3 and not t.prev else 1
            return {4: 5, 5: 3}[j]

        def taken_step(t, j):
            if t.nxt:
                return 2 if j in (2, 3) and not t.prev else 1
            return 4

        def bank_free_at(t, j):
            return pj_taken_at(t, j) - (1 if t.nxt else 3)

        def aux_at(t, k):
            return 3 * t.batch(1) + (k + 3)

        def head(t, s):
            d = s // H
            return (d, s % H) if t.has(d) else (None, None)

        first = Slot(0, -1, False, False, True)
        second = Slot(0, 0, False, True, True)

        def pair(i):
            a = Slot(i, 1, True, True, True)
            return a, Slot(i, 2, True, True, True)

        last = Slot(0, NB - 1, True, True, False)
        tail = Slot(0, NB, True, False, False)
        LOOPS = (NB - 2) // 2

        def run(eng, slot):
            slot(first)
            slot(second)
            with eng.Fori(0, LOOPS) as i:
                for t in pair(i):
                    slot(t)
            slot(last)
            slot(tail)

        block = ctx.enter_context(nc.Block())

        @block.sync
        def _(sp):
            def load_w(w, w_d):
                sp.dma_start(w_nat[:, w], w_d.rearrange("(o p) k -> p o k", p=P)).then_inc(w_in[w], 16)

            sp.dma_start(xs[:, 0], xv[0]).then_inc(x_in[0], 16)
            load_w(0, wq_d)
            load_w(1, wk_d)
            load_w(2, wv_d)
            sp.dma_start(xs[:, 1], xv[1]).then_inc(x_in[1], 16)
            sp.dma_start(adj_raw[:, 0], av[0]).then_inc(adj_in[0], 16)
            load_w(3, wo_d)
            for i in range(2):
                sp.sem_inc(out_done[i], 16 * NU)

            def stack(t, dst, blk, part, j, signal):
                sp.dma_start(dst[HD * blk:HD * blk + HD, t.par(1), j],
                             part[HD * j:HD * j + HD]).then_inc(signal, 16)

            def slot(t):
                if t.nxt:
                    sp.wait_ge(xn_ready, NU * t.batch(2))
                    sp.dma_start(xs[:, t.par(3)], xv[wrap(t, 3)]).then_inc(x_in[t.par(3)], 16)
                    need(sp, adj_scaled, t.batch(1))
                    need(sp, adj_checked, t.batch(1))
                    sp.dma_start(adj_raw[:, t.par(2)], av[wrap(t, 2)]).then_inc(adj_in[t.par(2)], 16)
                if t.cur:
                    sp.wait_ge(out_done[t.par(0)], 16 * NU * t.half(0) + 16 * NU)
                    sp.dma_start(x_res[:, t.par(0)], xv[t.batch(0)]).then_inc(xres_in[t.par(0)], 16)
                if t.nxt:
                    need(sp, scores_ready, H * t.batch(0))
                    sp.wait_ge(pj_hi, 4 * t.batch(1) + 2)
                    for blk in (0, 1):
                        for j in range(HC):
                            stack(t, q_stack, blk, q_hi, j, q_stacked)
                    for g in range(2):
                        sp.wait_ge(pj_taken[g], pj_taken_at(t, g))
                    for j in range(HC):
                        stack(t, q_stack, 2, q_lo, j, q_stacked)
                    for g in range(2):
                        sp.wait_ge(pj_taken[g], pj_taken_at(t, 2 + g))
                    for j in range(HC):
                        for blk, part in enumerate((k_hi, k_lo, k_hi)):
                            stack(t, k_stack, blk, part, j, k_stacked[j])
                if t.prev:
                    for u in range(NU):
                        sp.wait_ge(pj_taken[u], pj_taken_at(t, 4 + u))
                        sp.dma_start(ov[t.batch(-1)][:, u, :], x_res[:, t.par(-1), u, :])\
                          .then_inc(out_done[t.par(-1)], 16)

            def wrap(t, d):
                b = t.batch(d)
                return b % NB

            run(sp, slot)
            for i in range(2):
                sp.wait_ge(out_done[i], 16 * NU * (NB // 2 + 1))
                sp.wait_ge(x_in[i], 16 * (NB // 2 + 1))
                sp.wait_ge(adj_in[i], 16 * (NB // 2 + (i == 0)))

        @block.gpsimd
        def _(pool):
            g = nc.gpsimd
            g.memset(ident[:], 0.0).then_inc(consts_set, 1)
            g.memset(minus_half[:], -0.5).then_inc(consts_set, 1)
            pool.wait_ge(consts_set, 2)
            g.affine_select(out=ident[:], in_=ident[:], compare_op=ALU.not_equal, fill=1.0, base=0,
                            pattern=[[-1, P]], channel_multiplier=1).then_inc(ident_set, 1)
            pool.wait_ge(ident_set, 1)
            g.memset(ones_row[:], 1.0).then_inc(ones_set, 1)

            def layernorm(t, d):
                pool.wait_ge(ln_stats, NU * (t.batch(d) + 1))
                g.tensor_tensor(rstd[:], var_s[:], minus_half[:], ALU.pow).then_inc(rstd_ready, 1)
                pool.wait_ge(rstd_ready, t.batch(d) + 1)
                if d == 2:
                    pool.wait_ge(aux_full, aux_at(t, 1) - 3 if not t.first else 2)
                settle(pool)
                for u in range(NU):
                    g.tensor_scalar(xn[:, u, :], xs[:, t.par(d), u, :], neg_mean[:, u:u + 1],
                                    rstd[:, u:u + 1], ALU.add, ALU.mult).then_inc(xn_ready, 1)

            layernorm(first, 1)

            def scale_adj(t):
                pool.wait_ge(adj_in[t.par(1)], 16 * t.half(1) + 16)
                need(pool, logits_ready, NU * H * t.batch(0))
                settle(pool)
                g.tensor_scalar(adj_s[:, t.par(1)], adj_raw[:, t.par(1)], adj_scale[:, 0:1], 1.0,
                                ALU.mult, ALU.mult).then_inc(adj_scaled, 1)

            def spread(t, d, c):
                pool.wait_ge(recip_ready, NC * t.batch(d) + (c + 1))
                need(pool, rt_full, NC * t.batch(d) + c)
                settle(pool)
                g.tensor_copy(recip_wide[:], recip_kept[:].unsqueeze(3).broadcast_to([P, NU, HC, HD]))\
                 .then_inc(recip_spread, 1)

            def split_o(t, d, c):
                pool.wait_ge(o_norm_ready, NC * t.batch(d) + (c + 1))
                if c == 0:
                    pool.wait_ge(pj_full, NJ * t.batch(d) + 6)
                settle(pool)
                g.tensor_copy(o_hi[:, t.par(d), c, :], o_norm[:, c % 2, :]).then_inc(o_hi_ready, 1)
                pool.wait_ge(o_hi_ready, NC * t.batch(d) + (c + 1))
                g.tensor_tensor(o_lo[:, t.par(d), c, :], o_norm[:, c % 2, :], o_hi[:, t.par(d), c, :],
                                ALU.subtract).then_inc(o_split, 1)

            def slot(t):
                if t.first:
                    pool.wait_ge(scales_ready, 2)
                for s in range(H):
                    if s == 0 and t.nxt:
                        scale_adj(t)
                    if s == 2:
                        if t.prev:
                            split_o(t, -1, NC - 1)
                        if t.nxt:
                            layernorm(t, 2)
                    if s == 9 and t.nxt:
                        pool.wait_ge(pj_hi, 4 * t.batch(1) + 4)
                        g.tensor_tensor(k_diag[:], k_sum[:].unsqueeze(2).broadcast_to([P, NC, HC]),
                                        head_mask[:].unsqueeze(1).broadcast_to([P, NC, HC]), ALU.mult)\
                         .then_inc(k_diag_ready, 1)
                    if s % 4 == 3 and t.cur:
                        spread(t, 0, s // 4)
                    if s % 4 == 2 and s >= 6 and t.cur:
                        split_o(t, 0, s // 4 - 1)

            run(pool, slot)

        @block.scalar
        def _(act):
            a = nc.scalar
            def take_weights(w):
                act.wait_ge(scales_ready, w + 1)
                for kc in range(NC):
                    take_weight(w, kc, kc % W_BANKS)

            def take_weight(w, kc, bank):
                    act.wait_ge(wt_ready, NC * w + kc + 1)
                    a.activation(w_hi[:, w, kc, :], ps[:, bank, :], ACT.Copy, scale=w_scale[:, w:w + 1])\
                     .then_inc(wt_hi_taken, 1)

            def take_h(t, d, k, full):
                act.wait_ge(aux_full, full)
                a.activation(ht_hi[:, t.par(d), 2 * k:2 * k + 2, :],
                             ps[:, AUX_BANK, :].rearrange("p (c n) -> p c n", c=2), ACT.Relu)\
                 .then_inc(aux_hi, 1)

            take_h(first, 1, 0, 1)
            take_weights(0)
            take_h(first, 1, 1, 2)
            take_weights(1)

            def exp_rows(t, s):
                d, h = head(t, s)
                if d is None:
                    return
                need(act, pt_full, H * t.batch(d) + (h - 3))
                for u in range(NU):
                    act.wait_ge(logits_ready, NU * H * t.batch(d) + (NU * h + u + 1))
                    e = a.activation(probs[:, h % 4, u, :], logits[:, h % 4, u, :], ACT.Exp,
                                     bias=row_min[:, t.par(d), u, h:h + 1], scale=-1.0,
                                     accum_out=row_sum[:, t.par(d), u, h:h + 1])
                e.then_inc(probs_ready, 1)

            def take_probs_t(t, s):
                d, h = head(t, s)
                if d is None or h % 4 == 3:
                    return
                act.wait_ge(pt_full, H * t.batch(d) + (h + 1))
                need(act, pv_done, NC * t.batch(d) + (h // HC - 1))
                a.activation(probs_t[:, h % 8], ps[:, PT_BANK + h % 2, :].rearrange("p (m n) -> p m n", m=NU),
                             ACT.Copy).then_inc(pt_taken[h % 2], 1)

            def take_recip(t, d, c):
                act.wait_ge(rt_full, NC * t.batch(d) + (c + 1))
                need(act, o_norm_ready, NC * t.batch(d) + c)
                a.activation(recip_t[:], ps[:, PV_BANK, N:2 * N], ACT.Copy).then_inc(rt_taken, 1)

            def take_q(t, g):
                act.wait_ge(pj_full, pj_full_at(t, g))
                if g == 0:
                    need(act, q_stacked, 16 * NK * HC * t.batch(1))
                    if not t.first:
                        act.wait_ge(aux_full, aux_at(t, 2) - 3)
                a.activation(q_hi[:, 2 * g:2 * g + 2, :],
                             ps[:, PJ_BANK + g, :].rearrange("p (c n) -> p c n", c=2), ACT.Copy,
                             scale=-DOWN).then_inc(pj_hi, 1)

            def take_k(t, g):
                act.wait_ge(pj_full, pj_full_at(t, 2 + g))
                if g == 0:
                    need(act, scores_ready, H * t.batch(0) + HC if t.cur else 0)
                for c in range(2):
                    e = a.activation(k_hi[:, 2 * g + c, :], ps[:, PJ_BANK + g, N * c:N * c + N], ACT.Copy,
                                     scale=DOWN, accum_out=k_sum[:, 2 * g + c:2 * g + c + 1])
                e.then_inc(pj_hi, 1)

            def take_v(t, d, u):
                act.wait_ge(pj_full, NJ * t.batch(d) + (7 + u))
                if u == 0:
                    need(act, pv_done, NC * t.batch(d - 1))
                a.activation(v_sb[:, t.par(d), u, :], ps[:, PJ_BANK + u, :], ACT.Copy, scale=DOWN)\
                 .then_inc(pj_taken[u], 1)

            def slot(t):
                for s in range(H):
                    take_probs_t(t, s - 1)
                    if s == 0 and t.cur:
                        take_v(t, 0, 1)
                    if s == 2 and t.prev:
                        take_recip(t, -1, NC - 1)
                    if s % 4 == 2 and s >= 6 and t.cur:
                        take_recip(t, 0, s // 4 - 1)
                    if t.nxt:
                        if s in (2, 4):
                            take_q(t, s // 2 - 1)
                        if s in (6, 8):
                            take_k(t, s // 2 - 3)
                        if s in ((9, 12) if t.first else (7, 10)):
                            k = s // (12 if t.first else 10)
                            take_h(t, 2, k, aux_at(t, k))
                        if s == 14:
                            take_v(t, 1, 0)
                    if t.first and s == 8:
                        take_weights(2)
                    if t is second and 9 <= s < 9 + NC:
                        take_weight(3, s - 9, PJ_BANK + (s - 9) % 2)
                    exp_rows(t, s + 1)

            run(act, slot)

        @block.vector
        def _(dve):
            v = nc.vector
            v.memset(w_up[:], 2.0 ** W_UP).then_inc(consts_dve, 1)
            v.memset(head_mask[:], 0.0).then_inc(consts_dve, 1)
            dve.wait_ge(consts_dve, 2)
            v.memset(w_up[:, 1:2], K_UP * 2.0 ** W_UP).then_inc(consts_dve, 1)
            for j in range(HC):
                v.memset(head_mask[HD * j:HD * j + HD, j:j + 1], K_SUM_DOWN).then_inc(consts_dve, 1)
            dve.wait_ge(consts_dve, 3 + HC)

            def ln_statistics(t, d):
                dve.wait_ge(x_in[t.par(d)], 16 * t.half(d) + 16)
                step = (1 + 2 * NU) * t.batch(d)
                v.reduce_sum(x_sum[:], xs[:, t.par(d)], AX.X).then_inc(stat_step, 1)
                for u in range(NU):
                    v.bn_stats(stats[:, u, :], xs[:, t.par(d), u, :]).then_inc(stat_step, 1)
                for u in range(NU):
                    dve.wait_ge(stat_step, step + (u + 2))
                    settle(dve)
                    v.bn_aggr(mean_var[:, u, :], stats[:, u, :]).then_inc(stat_step, 1)
                dve.wait_ge(stat_step, step + (1 + 2 * NU))
                v.tensor_scalar(neg_mean[:], x_sum[:], -1.0 / D, None, ALU.mult).then_inc(ln_stats, 1)
                v.tensor_scalar(var_s[:], mean_var[:, :, 1], EPS, 2.0 ** (-2 * H_UP), ALU.add, ALU.mult)\
                 .then_inc(ln_stats, 1)

            def weight_max(w):
                dve.wait_ge(w_in[w], 16)
                v.tensor_reduce(out=w_max[:, w:w + 1], in_=w_nat[:, w].rearrange("p o k -> p (o k)"),
                                axis=AX.X, op=ALU.max, apply_absolute_value=True).then_inc(w_max_found, 1)

            def weight_row_max(w):
                dve.wait_ge(w_row_turned, w + 1)
                v.reduce_max(w_row_max[0:1, w:w + 1], ps[0:1, MAX_BANK, 0:P], AX.X).then_inc(w_row_max_found, 1)

            def weight_scale(w):
                one, step = slice(w, w + 1), 3 * w
                dve.wait_ge(w_top_found, w + 1)
                v.tensor_scalar(w_top[:, one], ps[:, MAX_BANK, TOP_COL + w:TOP_COL + w + 1],
                                2.0 ** (-20 if w < 2 else -60), None, ALU.max).then_inc(scale_step, 1)
                dve.wait_ge(scale_step, step + 1)
                v.tensor_scalar(w_pow[:, one].bitcast(I32), w_top[:, one].bitcast(I32), 0x7F800000, None,
                                ALU.bitwise_and).then_inc(scale_step, 1)
                dve.wait_ge(scale_step, step + 2)
                v.reciprocal(w_inv[:, one], w_pow[:, one]).then_inc(scale_step, 1)
                dve.wait_ge(scale_step, step + 3)
                if w == 1:
                    v.tensor_scalar(sigma[:], w_pow[:, 0:1], w_pow[:, 1:2], 2.0 ** -(2 * UP + 4),
                                    ALU.mult, ALU.mult)
                    v.tensor_scalar(adj_scale[:], w_inv[:, 0:1], w_inv[:, 1:2], -2.0 * 2.0 ** (2 * UP + 4),
                                    ALU.mult, ALU.mult)
                if w == 3:
                    v.tensor_scalar(out_scale[:], w_pow[:, 2:3], w_pow[:, 3:4], 2.0 ** -(UP + W_UP),
                                    ALU.mult, ALU.mult)
                v.tensor_tensor(w_scale[:, one], w_inv[:, one], w_up[:, one], ALU.mult)\
                 .then_inc(scales_ready, 1)

            def weight_rest(w):
                dve.wait_ge(scales_ready, w + 1)
                for kc in range(NC):
                    weight_chunk_rest(w, kc, kc % W_BANKS)

            def weight_chunk_rest(w, kc, bank):
                dve.wait_ge(wt_hi_taken, NC * w + kc + 1)
                v.scalar_tensor_tensor(out=w_lo[:, w, kc, :], in0=ps[:, bank, :],
                                       scalar=w_scale[:, w:w + 1], in1=w_hi[:, w, kc, :],
                                       op0=ALU.mult, op1=ALU.subtract).then_inc(wt_taken, 1)

            def take_h(t, d, k, n_hi):
                dve.wait_ge(aux_hi, n_hi)
                two = ps[:, AUX_BANK, :].rearrange("p (c n) -> p c n", c=2)
                v.scalar_tensor_tensor(out=ht_lo[:, t.par(d), 2 * k:2 * k + 2, :], in0=two, scalar=0.0,
                                       in1=ht_hi[:, t.par(d), 2 * k:2 * k + 2, :],
                                       op0=ALU.max, op1=ALU.subtract).then_inc(aux_taken, 1)

            ln_statistics(first, 1)
            weight_max(0)
            weight_row_max(0)
            weight_scale(0)
            take_h(first, 1, 0, 1)
            weight_max(1)
            weight_row_max(1)
            weight_rest(0)
            take_h(first, 1, 1, 2)
            weight_scale(1)
            weight_rest(1)

            def logit_rows(t, s):
                d, h = head(t, s)
                if d is None:
                    return
                dve.wait_ge(scores_ready, H * t.batch(d) + (h + 1))
                if h == 0:
                    dve.wait_ge(adj_scaled, t.batch(d) + 1)
                need(dve, probs_ready, H * t.batch(d) + (h - 3))
                settle(dve)
                for u in range(NU):
                    v.tensor_tensor_reduce(out=logits[:, h % 4, u, :], in0=ps[:, S_BANK + h % 2, N * u:N * u + N],
                                           in1=adj_s[:, t.par(d), u, :], scale=sigma[:, 0:1], scalar=3e38,
                                           op0=ALU.add, op1=ALU.min,
                                           accum_out=row_min[:, t.par(d), u, h:h + 1]).then_inc(logits_ready, 1)

            def take_probs_t(t, s):
                d, h = head(t, s)
                if d is None or h % 4 != 3:
                    return
                dve.wait_ge(pt_full, H * t.batch(d) + (h + 1))
                need(dve, pv_done, NC * t.batch(d) + (h // HC - 1))
                v.tensor_copy(probs_t[:, h % 8], ps[:, PT_BANK + h % 2, :].rearrange("p (m n) -> p m n", m=NU))\
                 .then_inc(pt_taken[h % 2], 1)

            def invert(t, d, c):
                hs = slice(HC * c, HC * c + HC)
                n = 2 * NC * t.batch(d) + 2 * c
                dve.wait_ge(probs_ready, H * t.batch(d) + HC * (c + 1))
                v.reciprocal(recip[:], row_sum[:, t.par(d), :, hs]).then_inc(recip_step, 1)
                v.scalar_tensor_tensor(out=some[:], in0=row_min[:, t.par(d), :, hs], scalar=0.0,
                                       in1=some_qk[:, t.par(d), :, hs], op0=ALU.not_equal, op1=ALU.max)\
                 .then_inc(recip_step, 1)
                dve.wait_ge(recip_step, n + 2)
                need(dve, recip_spread, NC * t.batch(d) + c)
                v.scalar_tensor_tensor(out=recip_kept[:], in0=some[:], scalar=0.0, in1=recip[:],
                                       op0=ALU.not_equal, op1=ALU.mult).then_inc(recip_ready, 1)

            def normalize(t, d, c):
                dve.wait_ge(pv_done, NC * t.batch(d) + (c + 1))
                dve.wait_ge(rt_taken, NC * t.batch(d) + (c + 1))
                need(dve, o_split, NC * t.batch(d) + (c - 1))
                v.tensor_tensor(o_norm[:, c % 2, :], ps[:, PV_BANK, 0:N], recip_t[:], ALU.mult)\
                 .then_inc(o_norm_ready, 1)

            def take_qk(t, j):
                dve.wait_ge(pj_hi, 4 * t.batch(1) + (j + 1))
                g = j % 2
                hi, lo = (q_hi, q_lo) if j < 2 else (k_hi, k_lo)
                v.scalar_tensor_tensor(out=lo[:, 2 * g:2 * g + 2, :].rearrange("p c n -> p (c n)"),
                                       in0=ps[:, PJ_BANK + g, :], scalar=-DOWN if j < 2 else DOWN,
                                       in1=hi[:, 2 * g:2 * g + 2, :].rearrange("p c n -> p (c n)"),
                                       op0=ALU.mult, op1=ALU.subtract).then_inc(pj_taken[g], taken_step(t, j))

            def check_adj(t):
                dve.wait_ge(adj_in[t.par(1)], 16 * t.half(1) + 16)
                v.tensor_reduce(out=adj_max[:, t.par(1), :], in_=adj_raw[:, t.par(1)], axis=AX.X, op=ALU.max,
                                apply_absolute_value=True).then_inc(adj_checked, 1)

            def test_rows(t):
                dve.wait_ge(aux_full, aux_at(t, 2))
                dve.wait_ge(adj_checked, t.batch(1) + 1)
                v.scalar_tensor_tensor(out=some_qk[:, t.par(1)],
                                       in0=ps[:, AUX_BANK, 0:NU * H].rearrange("p (u h) -> p u h", u=NU),
                                       scalar=0.0,
                                       in1=adj_max[:, t.par(1), :].unsqueeze(2).broadcast_to([P, NU, H]),
                                       op0=ALU.not_equal, op1=ALU.max).then_inc(aux_taken, 1)

            def residual(t, u):
                dve.wait_ge(pj_full, pj_full_at(t, 4 + u))
                dve.wait_ge(xres_in[t.par(-1)], 16 * t.half(-1) + 16)
                v.scalar_tensor_tensor(out=x_res[:, t.par(-1), u, :], in0=ps[:, PJ_BANK + u, :],
                                       scalar=out_scale[:, 0:1], in1=x_res[:, t.par(-1), u, :],
                                       op0=ALU.mult, op1=ALU.add).then_inc(pj_taken[u], taken_step(t, 4 + u))

            def slot(t):
                for s in range(H):
                    logit_rows(t, s + 1)
                    take_probs_t(t, s - 1)
                    if s % 4 == 3 and t.cur:
                        invert(t, 0, s // 4)
                    if s == 2 and t.prev:
                        normalize(t, -1, NC - 1)
                    if s % 4 == 2 and s >= 6 and t.cur:
                        normalize(t, 0, s // 4 - 1)
                    if t.nxt:
                        if s == (5 if t.first else 1):
                            ln_statistics(t, 2)
                        if s in (2, 4, 6, 8):
                            take_qk(t, s // 2 - 1)
                        if s == 5:
                            check_adj(t)
                        if s in ((9, 12) if t.first else (7, 10)):
                            k = s // (12 if t.first else 10)
                            take_h(t, 2, k, 2 * t.batch(2) + (k + 1))
                        if s == 14:
                            test_rows(t)
                    if t.prev and s in (10, 12):
                        residual(t, (s - 10) // 2)
                    if t.first:
                        if s == 3:
                            weight_max(2)
                        if s == 6:
                            weight_row_max(2)
                        if s == 7:
                            weight_scale(2)
                        if s == 8:
                            weight_rest(2)
                        if s == 10:
                            weight_max(3)
                        if s == 14:
                            weight_row_max(3)
                        if s == 15:
                            weight_scale(3)
                    if t is second and 9 <= s < 9 + NC:
                        weight_chunk_rest(3, s - 9, PJ_BANK + (s - 9) % 2)

            run(dve, slot)

        @block.tensor
        def _(pe):
            mm, tr = nc.tensor.matmul, nc.tensor.transpose
            pe.wait_ge(ident_set, 1)

            def turn_h(t, d, k, n):
                pe.wait_ge(xn_ready, NU * (t.batch(d) + 1))
                need(pe, aux_taken, n - 1)
                for c in range(2):
                    for u in range(NU):
                        m = tr(ps[:, AUX_BANK, N * c + P * u:N * c + P * u + P],
                               xn[:, u, P * (2 * k + c):P * (2 * k + c) + P], ident[:])
                m.then_inc(aux_full, 1)

            def turn_weights(w, chunks=range(NC)):
                pe.wait_ge(w_in[w], 16)
                for kc in chunks:
                    n = NC * w + kc
                    need(pe, wt_taken, n - (W_BANKS - 1))
                    for o in range(NC):
                        m = tr(ps[:, n % W_BANKS, P * o:P * o + P], w_nat[:, w, o, P * kc:P * kc + P], ident[:])
                    m.then_inc(wt_ready, 1)

            def turn_max(w):
                pe.wait_ge(w_max_found, w + 1)
                need(pe, scale_step, 3 * w)
                tr(ps[0:1, MAX_BANK, 0:P], w_max[:, w:w + 1], ident[:]).then_inc(w_row_turned, 1)

            def spread_max(w):
                pe.wait_ge(ones_set, 1)
                pe.wait_ge(w_row_max_found, w + 1)
                mm(ps[:, MAX_BANK, TOP_COL + w:TOP_COL + w + 1], ones_row[:], w_row_max[0:1, w:w + 1],
                   start=True, stop=True).then_inc(w_top_found, 1)

            def turn_last_weights(kc):
                if kc < 2:
                    pe.wait_ge(pj_taken[kc], bank_free_at(second, 4 + kc))
                else:
                    pe.wait_ge(wt_taken, NC * 3 + kc - 1)
                for o in range(NC):
                    m = tr(ps[:, PJ_BANK + kc % 2, P * o:P * o + P], w_nat[:, 3, o, P * kc:P * kc + P], ident[:])
                m.then_inc(wt_ready, 1)

            turn_weights(0, (0, 1))
            turn_max(0)
            turn_h(first, 1, 0, 1)
            spread_max(0)
            turn_weights(0, (2, 3))
            turn_h(first, 1, 1, 2)
            turn_max(1)
            spread_max(1)
            turn_weights(1)

            THREE = ((0, 0), (0, 1), (1, 0))
            W = (w_hi, w_lo)
            HT = (ht_hi, ht_lo)
            O = (o_hi, o_lo)

            def part_products(t, j):
                out = []
                g = j % 2
                if j < 4:
                    w = j // 2
                    for c in range(2):
                        steps = [(kc, a, b) for kc in range(NC) for a, b in THREE]
                        for i, (kc, a, b) in enumerate(steps):
                            fs = P * (2 * g + c)
                            out.append((ps[:, PJ_BANK + g, N * c:N * c + N], W[a][:, w, kc, fs:fs + P],
                                        HT[b][:, t.par(1), kc, :], i == 0, i == len(steps) - 1))
                elif j < 6:
                    steps = [(c, a, b) for c in range(NC) for a, b in THREE]
                    for i, (c, a, b) in enumerate(steps):
                        out.append((ps[:, PJ_BANK + g, :], O[a][:, t.par(-1), c, P * g:P * g + P],
                                    W[b][:, 3, c, :], i == 0, i == len(steps) - 1))
                else:
                    steps = [(kc, a, b) for kc in range(NC) for a, b in THREE]
                    for i, (kc, a, b) in enumerate(steps):
                        out.append((ps[:, PJ_BANK + g, :], HT[a][:, t.par(1), kc, P * g:P * g + P],
                                    W[b][:, 2, kc, :], i == 0, i == len(steps) - 1))
                return out

            def project_last(t, d, c):
                pe.wait_ge(o_split, NC * t.batch(d) + (c + 1))
                for u in range(NU):
                    if c == 0:
                        pe.wait_ge(pj_taken[u], bank_free_at(tail, 4 + u))
                    for k, (a, b) in enumerate(THREE):
                        m = mm(ps[:, PJ_BANK + u, :], O[a][:, t.par(d), c, P * u:P * u + P], W[b][:, 3, c, :],
                               start=(c == 0 and k == 0), stop=(c == NC - 1 and k == len(THREE) - 1))
                    if c == NC - 1:
                        m.then_inc(pj_full, full_step(tail, 4 + u))

            def project(t, s):
                j, part = s // 2, s % 2
                if not t.uses(j) or t is tail:
                    return
                if part == 0:
                    need(pe, pj_taken[j % 2], bank_free_at(t, j))
                    if j == 0:
                        pe.wait_ge(aux_taken, 2 if t.first else aux_at(t, 1) - 3)
                    if j == 4:
                        pe.wait_ge(o_split, NC * t.batch(0))
                    if t.first and j in (0, 2, 6):
                        pe.wait_ge(wt_taken, NC * (1 + {0: 0, 2: 1, 6: 2}[j]))
                    if t is second and j in (6, 7):
                        pe.wait_ge(wt_taken, NC * 3 + NC - 7 + j)
                products = part_products(t, j)
                half = len(products) // 2
                for o, l, r, start, stop in products[half * part:half * part + half]:
                    m = mm(o, l, r, start=start, stop=stop)
                if part == 1:
                    m.then_inc(pj_full, full_step(t, j))

            def scores(t, s):
                d, h = head(t, s)
                if d is None:
                    return
                c, j = h // HC, h % HC
                if h == 0:
                    pe.wait_ge(q_stacked, 16 * NK * HC * (t.batch(d) + 1))
                if h < HC:
                    pe.wait_ge(k_stacked[j], 16 * NK * (t.batch(d) + 1))
                need(pe, logits_ready, NU * (H * t.batch(d) + (h - 1)))
                for u in range(NU):
                    m = mm(ps[:, S_BANK + h % 2, N * u:N * u + N], q_stack[:, t.par(d), j, c, P * u:P * u + P],
                           k_stack[:, t.par(d), j, c, :], start=True, stop=True)
                m.then_inc(scores_ready, 1)

            def turn_probs(t, s):
                d, h = head(t, s)
                if d is None:
                    return
                pe.wait_ge(probs_ready, H * t.batch(d) + (h + 1))
                need(pe, pt_taken[h % 2], (H // 2) * t.batch(d) + h // 2)
                for mh in range(NU):
                    for u in range(NU):
                        m = tr(ps[:, PT_BANK + h % 2, N * mh + P * u:N * mh + P * u + P],
                               probs[:, h % 4, u, P * mh:P * mh + P], ident[:])
                m.then_inc(pt_full, 1)

            def values(t, d, c):
                for i in range(2):
                    pe.wait_ge(pt_taken[i], (H // 2) * t.batch(d) + 2 * (c + 1))
                need(pe, o_norm_ready, NC * t.batch(d) + c)
                if t is second and c == 0:
                    pe.wait_ge(scale_step, 3 * 3 + 1)
                if c == 0:
                    for u in range(NU):
                        pe.wait_ge(pj_taken[u], (NJ // 2) * (t.batch(d) + 1))
                for mh in range(NU):
                    for j in range(HC):
                        h = HC * c + j
                        m = mm(ps[HD * j:HD * j + HD, PV_BANK, 0:N],
                               v_sb[:, t.par(d), mh, HD * h:HD * h + HD], probs_t[:, h % 8, mh, :],
                               start=(mh == 0), stop=(mh == NU - 1))
                m.then_inc(pv_done, 1)

            def turn_recip(t, d, c):
                pe.wait_ge(recip_spread, NC * t.batch(d) + (c + 1))
                for u in range(NU):
                    m = tr(ps[:, PV_BANK, N + P * u:N + P * u + P],
                           recip_wide[:, u].rearrange("p j f -> p (j f)"), ident[:])
                m.then_inc(rt_full, 1)

            def row_test(t):
                pe.wait_ge(k_diag_ready, t.batch(1) + 1)
                pe.wait_ge(aux_taken, aux_at(t, 2) - 1)
                for u in range(NU):
                    for c in range(NC):
                        m = mm(ps[:, AUX_BANK, H * u + HC * c:H * u + HC * c + HC],
                               q_hi[:, c, P * u:P * u + P], k_diag[:, c, :], start=True, stop=True)
                m.then_inc(aux_full, 1)

            def slot(t):
                for s in range(H):
                    if t.first:
                        if s == 8:
                            turn_max(2)
                            spread_max(2)
                            turn_weights(2)
                        if s == 14:
                            turn_max(3)
                        if s == 15:
                            spread_max(3)
                    if t.first and s == H - 2:
                        pe.wait_ge(wt_taken, 3 * NC)
                    scores(t, s + 2)
                    if s == 1 and t.prev:
                        turn_recip(t, -1, NC - 1)
                    if t.cur and s >= 4 and s % 4 == 1:
                        turn_recip(t, 0, s // 4 - 1)
                    project(t, s)
                    turn_probs(t, s)
                    if t.nxt:
                        if s in ((9, 12) if t.first else (6, 9)):
                            turn_h(t, 2, s // 9 if not t.first else s // 12, aux_at(t, s // (12 if t.first else 9)))
                        if s == 13:
                            row_test(t)
                    if s == 0 and t.prev:
                        values(t, -1, NC - 1)
                    if t.cur and s >= 4 and s % 4 == 0:
                        values(t, 0, s // 4 - 1)
                    if t is second and 8 <= s < 8 + NC:
                        turn_last_weights(s - 8)
                    if t is last and s in (13, 14, 15):
                        project_last(t, 0, s - 13)
                    if t is tail and s == 2:
                        project_last(t, -1, NC - 1)

            run(pe, slot)


_INS = ["x", "adj", "L0_gnn_Wq", "L0_gnn_Wk", "L0_gnn_Wv", "L0_gnn_Wo"]


def kernel(**inputs):
    import numpy as _np
    import concourse.bacc as _bacc
    from concourse import mybir as _mybir
    from concourse.bass_utils import run_bass_kernel_spmd as _run

    nc = _bacc.Bacc("TRN2", target_bir_lowering=False, num_devices=1)
    arrays, args = {}, []
    for name in _INS:
        a = _np.ascontiguousarray(inputs[name])
        arrays[f"in_{name}"] = a
        args.append(nc.dram_tensor(f"in_{name}", a.shape, _mybir.dt.from_np(a.dtype), kind="ExternalInput").ap())
    out = nc.dram_tensor("out_0", inputs["x"].shape, _mybir.dt.float32, kind="ExternalOutput").ap()
    emit(nc, *args, out)
    return _run(nc, [arrays], core_ids=[0]).results[0]["out_0"]
```

```python
import concourse.bass as bass
from concourse import mybir
from contextlib import ExitStack

F32 = mybir.dt.float32
F16 = mybir.dt.float16
I32 = mybir.dt.int32
ACT = mybir.ActivationFunctionType
ALU = mybir.AluOpType
AX = mybir.AxisListType

NB, N, D, H = 32, 256, 512, 16
HD = D // H
P = 128
NU = N // P
NC = D // P
HC = P // HD
NK = 3

EPS = 1e-5
H_UP = 10
W_UP = 14
DOWN = 2.0 ** -19
UP = H_UP + W_UP - 19
K_UP = 16.0 * D ** -0.5
K_SUM_DOWN = 1.0 / N

JOBS = ("q01", "q23", "k01", "k23", "o0", "o1", "v0", "v1")
NJ = len(JOBS)


class Slot:

    def __init__(self, i, off, prev, cur, nxt):
        self.i, self.off = i, off
        self.prev, self.cur, self.nxt = prev, cur, nxt
        self.first = i == 0 and off == -1 if isinstance(i, int) else False

    def batch(self, d):
        return 2 * self.i + (self.off + d)

    def par(self, d):
        return (self.off + d) % 2

    def half(self, d):
        return self.i + (self.off + d) // 2

    def has(self, d):
        return {-1: self.prev, 0: self.cur, 1: self.nxt}[d]

    def uses(self, j):
        return self.prev if j in (4, 5) else self.nxt


def emit(nc, x_d, adj_d, wq_d, wk_d, wv_d, wo_d, out_d):
    xv = x_d.rearrange("b (u p) d -> b p u d", p=P)
    av = adj_d.rearrange("b (u p) m -> b p u m", p=P)
    ov = out_d.rearrange("b (u p) d -> b p u d", p=P)

    ctx = ExitStack()
    with ctx:
        def sb(name, shape, dt=F32):
            return ctx.enter_context(nc.sbuf_tensor(name, shape, dt))

        def sem(name):
            return ctx.enter_context(nc.semaphore(name))

        ident = sb("ident", [P, P])
        head_mask = sb("head_mask", [P, HC])
        w_nat = sb("w_nat", [P, 4, NC, D])
        w_hi = sb("w_hi", [P, 4, NC, D], F16)
        w_lo = sb("w_lo", [P, 4, NC, D], F16)
        w_max = sb("w_max", [P, 4])
        w_row_max = sb("w_row_max", [1, 4])
        ones_row = sb("ones_row", [1, P])
        w_top = sb("w_top", [P, 4])
        w_pow = sb("w_pow", [P, 4])
        w_inv = sb("w_inv", [P, 4])
        w_up = sb("w_up", [P, 4])
        w_scale = sb("w_scale", [P, 4])
        sigma = sb("sigma", [P, 1])
        adj_scale = sb("adj_scale", [P, 1])
        out_scale = sb("out_scale", [P, 1])
        xs = sb("xs", [P, 2, NU, D])
        xn = sb("xn", [P, NU, D])
        x_res = sb("x_res", [P, 2, NU, D])
        adj_raw = sb("adj_raw", [P, 2, NU, N])
        adj_s = sb("adj_s", [P, 2, NU, N])
        adj_max = sb("adj_max", [P, 2, NU])
        x_sum = sb("x_sum", [P, NU])
        stats = sb("stats", [P, NU, 6])
        mean_var = sb("mean_var", [P, NU, 2])
        neg_mean = sb("neg_mean", [P, NU])
        var_s = sb("var_s", [P, NU])
        rstd = sb("rstd", [P, NU])
        minus_half = sb("minus_half", [P, NU])
        ht_hi = sb("ht_hi", [P, 2, NC, N], F16)
        ht_lo = sb("ht_lo", [P, 2, NC, N], F16)
        q_hi = sb("q_hi", [P, NC, N], F16)
        q_lo = sb("q_lo", [P, NC, N], F16)
        k_hi = sb("k_hi", [P, NC, N], F16)
        k_lo = sb("k_lo", [P, NC, N], F16)
        k_sum = sb("k_sum", [P, NC])
        k_diag = sb("k_diag", [P, NC, HC], F16)
        q_stack = sb("q_stack", [NK * HD, 2, HC, NC, N], F16)
        k_stack = sb("k_stack", [NK * HD, 2, HC, NC, N], F16)
        v_sb = sb("v_sb", [P, 2, NU, D])
        logits = sb("logits", [P, 4, NU, N])
        probs = sb("probs", [P, 4, NU, N])
        row_min = sb("row_min", [P, 2, NU, H])
        row_sum = sb("row_sum", [P, 2, NU, H])
        some_qk = sb("some_qk", [P, 2, NU, H])
        some = sb("some", [P, 4, NU])
        recip = sb("recip", [P, 4, NU])
        probs_t = sb("probs_t", [P, 8, NU, N])
        o_hi = sb("o_hi", [P, 2, NC, N], F16)
        o_lo = sb("o_lo", [P, 2, NC, N], F16)

        ps = ctx.enter_context(nc.psum_tensor("ps", [P, 8, 512], F32))
        S_BANK, PT_BANK, PV_BANK, PJ_BANK, AUX_BANK = 0, 2, 4, 5, 7
        W_BANKS, TOP_COL = 4, P

        def max_bank(w):
            return PV_BANK if w < 3 else AUX_BANK

        waits_met = sem("waits_met")
        w_in = [sem(f"w_in{w}") for w in range(4)]
        x_in = [sem(f"x_in{i}") for i in range(2)]
        adj_in = [sem(f"adj_in{i}") for i in range(2)]
        xres_in = [sem(f"xres_in{i}") for i in range(2)]
        out_done = [sem(f"out_done{i}") for i in range(2)]
        q_stacked = sem("q_stacked")
        k_stacked = [sem(f"k_stacked{j}") for j in range(HC)]
        consts_set = sem("consts_set")
        ident_set = sem("ident_set")
        consts_dve = sem("consts_dve")
        w_max_found = sem("w_max_found")
        ones_set = sem("ones_set")
        w_row_turned = sem("w_row_turned")
        w_row_max_found = sem("w_row_max_found")
        w_top_found = sem("w_top_found")
        scale_step = sem("scale_step")
        scales_ready = sem("scales_ready")
        wt_ready = sem("wt_ready")
        wt_hi_taken = sem("wt_hi_taken")
        wt_taken = sem("wt_taken")
        stat_step = sem("stat_step")
        ln_stats = sem("ln_stats")
        rstd_ready = sem("rstd_ready")
        xn_ready = sem("xn_ready")
        adj_scaled = sem("adj_scaled")
        adj_checked = sem("adj_checked")
        aux_full = sem("aux_full")
        aux_hi = sem("aux_hi")
        aux_taken = sem("aux_taken")
        pj_full = sem("pj_full")
        pj_hi = sem("pj_hi")
        pj_taken = [sem(f"pj_taken{i}") for i in range(2)]
        k_diag_ready = sem("k_diag_ready")
        scores_ready = sem("scores_ready")
        logits_ready = sem("logits_ready")
        probs_ready = sem("probs_ready")
        pt_full = sem("pt_full")
        pt_taken = [sem(f"pt_taken{i}") for i in range(2)]
        pv_done = sem("pv_done")
        rows_tested = sem("rows_tested")
        recip_ready = sem("recip_ready")
        probs_scaled = sem("probs_scaled")
        o_hi_ready = sem("o_hi_ready")
        o_split = sem("o_split")

        def need(eng, s, value):
            if isinstance(value, int) and value <= 0:
                return
            eng.wait_ge(s, value)

        def settle(eng):
            eng.sem_inc(waits_met, 1)

        def pj_full_at(t, j):
            return NJ * t.batch(1) + (j + 1)

        def pj_taken_at(t, j):
            return (NJ // 2) * t.batch(1) + (j // 2 + 1)

        def full_step(t, j):
            if t.nxt:
                return 3 if j == 3 and not t.prev else 1
            return {4: 5, 5: 3}[j]

        def taken_step(t, j):
            if t.nxt:
                return 2 if j in (2, 3) and not t.prev else 1
            return 4

        def bank_free_at(t, j):
            return pj_taken_at(t, j) - (1 if t.nxt else 3)

        def aux_at(t, k):
            return 3 * t.batch(1) + (k + 3)

        def head(t, s):
            d = s // H
            return (d, s % H) if t.has(d) else (None, None)

        def turn_h_steps(t):
            return (9, 12) if t.first else (7, 10)

        def take_h_steps(t):
            return (9, 12) if t.first else (8, 11)

        def residual_steps(t):
            return (6, 8) if t is last else (10, 12)

        WO_STEP = 7

        first = Slot(0, -1, False, False, True)
        second = Slot(0, 0, False, True, True)

        def pair(i):
            a = Slot(i, 1, True, True, True)
            return a, Slot(i, 2, True, True, True)

        last = Slot(0, NB - 1, True, True, False)
        tail = Slot(0, NB, True, False, False)
        LOOPS = (NB - 2) // 2

        def run(eng, slot):
            slot(first)
            slot(second)
            with eng.Fori(0, LOOPS) as i:
                for t in pair(i):
                    slot(t)
            slot(last)
            slot(tail)

        block = ctx.enter_context(nc.Block())

        @block.sync
        def _(sp):
            def load_w(w, w_d):
                sp.dma_start(w_nat[:, w], w_d.rearrange("(o p) k -> p o k", p=P)).then_inc(w_in[w], 16)

            sp.dma_start(xs[:, 0], xv[0]).then_inc(x_in[0], 16)
            load_w(0, wq_d)
            load_w(1, wk_d)
            load_w(2, wv_d)
            sp.dma_start(xs[:, 1], xv[1]).then_inc(x_in[1], 16)
            sp.dma_start(adj_raw[:, 0], av[0]).then_inc(adj_in[0], 16)
            load_w(3, wo_d)
            for i in range(2):
                sp.sem_inc(out_done[i], 16 * NU)

            def stack(t, dst, blk, part, j, signal):
                sp.dma_start(dst[HD * blk:HD * blk + HD, t.par(1), j],
                             part[HD * j:HD * j + HD]).then_inc(signal, 16)

            def slot(t):
                if t.nxt:
                    sp.wait_ge(xn_ready, NU * t.batch(2))
                    sp.dma_start(xs[:, t.par(3)], xv[wrap(t, 3)]).then_inc(x_in[t.par(3)], 16)
                    need(sp, adj_scaled, t.batch(1))
                    need(sp, adj_checked, t.batch(1))
                    sp.dma_start(adj_raw[:, t.par(2)], av[wrap(t, 2)]).then_inc(adj_in[t.par(2)], 16)
                if t.cur:
                    sp.wait_ge(out_done[t.par(0)], 16 * NU * t.half(0) + 16 * NU)
                    sp.dma_start(x_res[:, t.par(0)], xv[t.batch(0)]).then_inc(xres_in[t.par(0)], 16)
                if t.nxt:
                    need(sp, scores_ready, H * t.batch(0))
                    sp.wait_ge(pj_hi, 4 * t.batch(1) + 2)
                    for blk in (0, 1):
                        for j in range(HC):
                            stack(t, q_stack, blk, q_hi, j, q_stacked)
                    for g in range(2):
                        sp.wait_ge(pj_taken[g], pj_taken_at(t, g))
                    for j in range(HC):
                        stack(t, q_stack, 2, q_lo, j, q_stacked)
                    for g in range(2):
                        sp.wait_ge(pj_taken[g], pj_taken_at(t, 2 + g))
                    for j in range(HC):
                        for blk, part in enumerate((k_hi, k_lo, k_hi)):
                            stack(t, k_stack, blk, part, j, k_stacked[j])
                if t.prev:
                    for u in range(NU):
                        sp.wait_ge(pj_taken[u], pj_taken_at(t, 4 + u))
                        sp.dma_start(ov[t.batch(-1)][:, u, :], x_res[:, t.par(-1), u, :])\
                          .then_inc(out_done[t.par(-1)], 16)

            def wrap(t, d):
                b = t.batch(d)
                return b % NB

            run(sp, slot)
            for i in range(2):
                sp.wait_ge(out_done[i], 16 * NU * (NB // 2 + 1))
                sp.wait_ge(x_in[i], 16 * (NB // 2 + 1))
                sp.wait_ge(adj_in[i], 16 * (NB // 2 + (i == 0)))

        @block.gpsimd
        def _(pool):
            g = nc.gpsimd
            g.memset(ident[:], 0.0).then_inc(consts_set, 1)
            g.memset(minus_half[:], -0.5).then_inc(consts_set, 1)
            pool.wait_ge(consts_set, 2)
            g.affine_select(out=ident[:], in_=ident[:], compare_op=ALU.not_equal, fill=1.0, base=0,
                            pattern=[[-1, P]], channel_multiplier=1).then_inc(ident_set, 1)
            pool.wait_ge(ident_set, 1)
            g.memset(ones_row[:], 1.0).then_inc(ones_set, 1)

            def layernorm(t, d):
                pool.wait_ge(ln_stats, NU * (t.batch(d) + 1))
                g.tensor_tensor(rstd[:], var_s[:], minus_half[:], ALU.pow).then_inc(rstd_ready, 1)
                pool.wait_ge(rstd_ready, t.batch(d) + 1)
                if d == 2:
                    pool.wait_ge(aux_full, aux_at(t, 1) - 3 if not t.first else 2)
                settle(pool)
                for u in range(NU):
                    g.tensor_scalar(xn[:, u, :], xs[:, t.par(d), u, :], neg_mean[:, u:u + 1],
                                    rstd[:, u:u + 1], ALU.add, ALU.mult).then_inc(xn_ready, 1)

            layernorm(first, 1)

            def scale_adj(t):
                pool.wait_ge(adj_in[t.par(1)], 16 * t.half(1) + 16)
                need(pool, logits_ready, NU * H * t.batch(0))
                settle(pool)
                g.tensor_scalar(adj_s[:, t.par(1)], adj_raw[:, t.par(1)], adj_scale[:, 0:1], 1.0,
                                ALU.mult, ALU.mult).then_inc(adj_scaled, 1)

            def scale_probs(t, s):
                d, h = head(t, s)
                if d is None:
                    return
                pool.wait_ge(recip_ready, 2 * (H * t.batch(d) + (h + 1)))
                settle(pool)
                for u in range(NU):
                    e = g.tensor_scalar(probs[:, h % 4, u, :], probs[:, h % 4, u, :], recip[:, h % 4, u:u + 1],
                                        some[:, h % 4, u:u + 1], ALU.mult, ALU.mult)
                e.then_inc(probs_scaled, 1)

            def slot(t):
                if t.first:
                    pool.wait_ge(scales_ready, 2)
                for s in range(H):
                    if s == 0 and t.nxt:
                        scale_adj(t)
                    scale_probs(t, s + 1)
                    if s == 4 and t.nxt:
                        layernorm(t, 2)
                    if s == 9 and t.nxt:
                        pool.wait_ge(pj_hi, 4 * t.batch(1) + 4)
                        g.tensor_tensor(k_diag[:], k_sum[:].unsqueeze(2).broadcast_to([P, NC, HC]),
                                        head_mask[:].unsqueeze(1).broadcast_to([P, NC, HC]), ALU.mult)\
                         .then_inc(k_diag_ready, 1)

            run(pool, slot)

        @block.scalar
        def _(act):
            a = nc.scalar

            def take_weights(w):
                act.wait_ge(scales_ready, w + 1)
                for kc in range(NC):
                    take_weight(w, kc, kc % W_BANKS)

            def take_weight(w, kc, bank):
                act.wait_ge(wt_ready, NC * w + kc + 1)
                a.activation(w_hi[:, w, kc, :], ps[:, bank, :], ACT.Copy, scale=w_scale[:, w:w + 1])\
                 .then_inc(wt_hi_taken, 1)

            def take_h(t, d, k, full):
                act.wait_ge(aux_full, full)
                a.activation(ht_hi[:, t.par(d), 2 * k:2 * k + 2, :],
                             ps[:, AUX_BANK, :].rearrange("p (c n) -> p c n", c=2), ACT.Relu)\
                 .then_inc(aux_hi, 1)

            take_h(first, 1, 0, 1)
            take_weights(0)
            take_h(first, 1, 1, 2)
            take_weights(1)

            def exp_rows(t, s):
                d, h = head(t, s)
                if d is None:
                    return
                need(act, pt_full, H * t.batch(d) + (h - 3))
                for u in range(NU):
                    act.wait_ge(logits_ready, NU * H * t.batch(d) + (NU * h + u + 1))
                    e = a.activation(probs[:, h % 4, u, :], logits[:, h % 4, u, :], ACT.Exp,
                                     bias=row_min[:, t.par(d), u, h:h + 1], scale=-1.0,
                                     accum_out=row_sum[:, t.par(d), u, h:h + 1])
                e.then_inc(probs_ready, 1)

            def take_probs_t(t, s):
                d, h = head(t, s)
                if d is None or h % 4 == 3:
                    return
                act.wait_ge(pt_full, H * t.batch(d) + (h + 1))
                need(act, pv_done, NC * t.batch(d) + (h // HC - 1))
                a.activation(probs_t[:, h % 8], ps[:, PT_BANK + h % 2, :].rearrange("p (m n) -> p m n", m=NU),
                             ACT.Copy).then_inc(pt_taken[h % 2], 1)

            def take_o(t, d, c):
                act.wait_ge(pv_done, NC * t.batch(d) + (c + 1))
                if c == 0:
                    act.wait_ge(pj_full, NJ * t.batch(d) + 6)
                a.activation(o_hi[:, t.par(d), c, :], ps[:, PV_BANK, 0:N], ACT.Copy).then_inc(o_hi_ready, 1)

            def take_q(t, g):
                act.wait_ge(pj_full, pj_full_at(t, g))
                if g == 0:
                    need(act, q_stacked, 16 * NK * HC * t.batch(1))
                    if not t.first:
                        act.wait_ge(aux_full, aux_at(t, 2) - 3)
                a.activation(q_hi[:, 2 * g:2 * g + 2, :],
                             ps[:, PJ_BANK + g, :].rearrange("p (c n) -> p c n", c=2), ACT.Copy,
                             scale=-DOWN).then_inc(pj_hi, 1)

            def take_k(t, g):
                act.wait_ge(pj_full, pj_full_at(t, 2 + g))
                if g == 0:
                    need(act, scores_ready, H * t.batch(0) + HC if t.cur else 0)
                for c in range(2):
                    e = a.activation(k_hi[:, 2 * g + c, :], ps[:, PJ_BANK + g, N * c:N * c + N], ACT.Copy,
                                     scale=DOWN, accum_out=k_sum[:, 2 * g + c:2 * g + c + 1])
                e.then_inc(pj_hi, 1)

            def take_v(t, d, u):
                act.wait_ge(pj_full, NJ * t.batch(d) + (7 + u))
                if u == 0:
                    need(act, pv_done, NC * t.batch(d - 1))
                a.activation(v_sb[:, t.par(d), u, :], ps[:, PJ_BANK + u, :], ACT.Copy, scale=DOWN)\
                 .then_inc(pj_taken[u], 1)

            def slot(t):
                for s in range(H):
                    take_probs_t(t, s - 1)
                    if s == 0 and t.cur:
                        take_v(t, 0, 1)
                    if t.nxt:
                        if s in (2, 4):
                            take_q(t, s // 2 - 1)
                        if s in (6, 8):
                            take_k(t, s // 2 - 3)
                        if s in take_h_steps(t):
                            k = take_h_steps(t).index(s)
                            take_h(t, 2, k, aux_at(t, k))
                        if s == 14:
                            take_v(t, 1, 0)
                    if t.first and s == 8:
                        take_weights(2)
                    if t is second and s - 1 in range(WO_STEP, WO_STEP + NC):
                        kc = s - 1 - WO_STEP
                        take_weight(3, kc, PJ_BANK + kc % 2)
                    exp_rows(t, s + 2)
                    if s == 1 and t.prev:
                        take_o(t, -1, NC - 1)
                    if s % 4 == 1 and s >= 4 and t.cur:
                        take_o(t, 0, s // 4 - 1)

            run(act, slot)

        @block.vector
        def _(dve):
            v = nc.vector
            v.memset(w_up[:], 2.0 ** W_UP).then_inc(consts_dve, 1)
            v.memset(head_mask[:], 0.0).then_inc(consts_dve, 1)
            dve.wait_ge(consts_dve, 2)
            v.memset(w_up[:, 1:2], K_UP * 2.0 ** W_UP).then_inc(consts_dve, 1)
            for j in range(HC):
                v.memset(head_mask[HD * j:HD * j + HD, j:j + 1], K_SUM_DOWN).then_inc(consts_dve, 1)
            dve.wait_ge(consts_dve, 3 + HC)

            def ln_sum(t, d):
                dve.wait_ge(x_in[t.par(d)], 16 * t.half(d) + 16)
                v.reduce_sum(x_sum[:], xs[:, t.par(d)], AX.X).then_inc(stat_step, 1)

            def ln_statistics(t, d, u):
                v.bn_stats(stats[:, u, :], xs[:, t.par(d), u, :]).then_inc(stat_step, 1)

            def ln_mean_var(t, d):
                step = (1 + 2 * NU) * t.batch(d)
                for u in range(NU):
                    dve.wait_ge(stat_step, step + (u + 2))
                    settle(dve)
                    v.bn_aggr(mean_var[:, u, :], stats[:, u, :]).then_inc(stat_step, 1)
                dve.wait_ge(stat_step, step + (1 + 2 * NU))
                v.tensor_scalar(neg_mean[:], x_sum[:], -1.0 / D, None, ALU.mult).then_inc(ln_stats, 1)
                v.tensor_scalar(var_s[:], mean_var[:, :, 1], EPS, 2.0 ** (-2 * H_UP), ALU.add, ALU.mult)\
                 .then_inc(ln_stats, 1)

            def weight_max(w):
                dve.wait_ge(w_in[w], 16)
                v.tensor_reduce(out=w_max[:, w:w + 1], in_=w_nat[:, w].rearrange("p o k -> p (o k)"),
                                axis=AX.X, op=ALU.max, apply_absolute_value=True).then_inc(w_max_found, 1)

            def weight_row_max(w):
                dve.wait_ge(w_row_turned, w + 1)
                v.reduce_max(w_row_max[0:1, w:w + 1], ps[0:1, max_bank(w), 0:P], AX.X).then_inc(w_row_max_found, 1)

            def weight_scale(w):
                one, step = slice(w, w + 1), 3 * w
                dve.wait_ge(w_top_found, w + 1)
                v.tensor_scalar(w_top[:, one], ps[:, max_bank(w), TOP_COL + w:TOP_COL + w + 1],
                                2.0 ** (-20 if w < 2 else -60), None, ALU.max).then_inc(scale_step, 1)
                dve.wait_ge(scale_step, step + 1)
                v.tensor_scalar(w_pow[:, one].bitcast(I32), w_top[:, one].bitcast(I32), 0x7F800000, None,
                                ALU.bitwise_and).then_inc(scale_step, 1)
                dve.wait_ge(scale_step, step + 2)
                v.reciprocal(w_inv[:, one], w_pow[:, one]).then_inc(scale_step, 1)
                dve.wait_ge(scale_step, step + 3)
                if w == 1:
                    v.tensor_scalar(sigma[:], w_pow[:, 0:1], w_pow[:, 1:2], 2.0 ** -(2 * UP + 4),
                                    ALU.mult, ALU.mult)
                    v.tensor_scalar(adj_scale[:], w_inv[:, 0:1], w_inv[:, 1:2], -2.0 * 2.0 ** (2 * UP + 4),
                                    ALU.mult, ALU.mult)
                if w == 3:
                    v.tensor_scalar(out_scale[:], w_pow[:, 2:3], w_pow[:, 3:4], 2.0 ** -(UP + W_UP),
                                    ALU.mult, ALU.mult)
                v.tensor_tensor(w_scale[:, one], w_inv[:, one], w_up[:, one], ALU.mult)\
                 .then_inc(scales_ready, 1)

            def weight_rest(w):
                dve.wait_ge(scales_ready, w + 1)
                for kc in range(NC):
                    weight_chunk_rest(w, kc, kc % W_BANKS)

            def weight_chunk_rest(w, kc, bank):
                dve.wait_ge(wt_hi_taken, NC * w + kc + 1)
                v.scalar_tensor_tensor(out=w_lo[:, w, kc, :], in0=ps[:, bank, :],
                                       scalar=w_scale[:, w:w + 1], in1=w_hi[:, w, kc, :],
                                       op0=ALU.mult, op1=ALU.subtract).then_inc(wt_taken, 1)

            def take_h(t, d, k, n_hi):
                dve.wait_ge(aux_hi, n_hi)
                two = ps[:, AUX_BANK, :].rearrange("p (c n) -> p c n", c=2)
                v.scalar_tensor_tensor(out=ht_lo[:, t.par(d), 2 * k:2 * k + 2, :], in0=two, scalar=0.0,
                                       in1=ht_hi[:, t.par(d), 2 * k:2 * k + 2, :],
                                       op0=ALU.max, op1=ALU.subtract).then_inc(aux_taken, 1)

            ln_sum(first, 1)
            for u in range(NU):
                ln_statistics(first, 1, u)
            ln_mean_var(first, 1)
            weight_max(0)
            weight_row_max(0)
            weight_scale(0)
            take_h(first, 1, 0, 1)
            weight_max(1)
            weight_row_max(1)
            weight_rest(0)
            take_h(first, 1, 1, 2)
            weight_scale(1)
            weight_rest(1)

            def logit_rows(t, s):
                d, h = head(t, s)
                if d is None:
                    return
                dve.wait_ge(scores_ready, H * t.batch(d) + (h + 1))
                if h == 0:
                    dve.wait_ge(adj_scaled, t.batch(d) + 1)
                need(dve, probs_ready, H * t.batch(d) + (h - 3))
                settle(dve)
                for u in range(NU):
                    v.tensor_tensor_reduce(out=logits[:, h % 4, u, :], in0=ps[:, S_BANK + h % 2, N * u:N * u + N],
                                           in1=adj_s[:, t.par(d), u, :], scale=sigma[:, 0:1], scalar=3e38,
                                           op0=ALU.add, op1=ALU.min,
                                           accum_out=row_min[:, t.par(d), u, h:h + 1]).then_inc(logits_ready, 1)

            def take_probs_t(t, s):
                d, h = head(t, s)
                if d is None or h % 4 != 3:
                    return
                dve.wait_ge(pt_full, H * t.batch(d) + (h + 1))
                need(dve, pv_done, NC * t.batch(d) + (h // HC - 1))
                v.tensor_copy(probs_t[:, h % 8], ps[:, PT_BANK + h % 2, :].rearrange("p (m n) -> p m n", m=NU))\
                 .then_inc(pt_taken[h % 2], 1)

            def invert(t, s):
                d, h = head(t, s)
                if d is None:
                    return
                if h == 0:
                    dve.wait_ge(rows_tested, 2 * (t.batch(d) + 1))
                dve.wait_ge(probs_ready, H * t.batch(d) + (h + 1))
                need(dve, probs_scaled, H * t.batch(d) + (h - 3))
                settle(dve)
                v.reciprocal(recip[:, h % 4, :], row_sum[:, t.par(d), :, h]).then_inc(recip_ready, 1)
                v.scalar_tensor_tensor(out=some[:, h % 4, :], in0=row_min[:, t.par(d), :, h], scalar=0.0,
                                       in1=some_qk[:, t.par(d), :, h], op0=ALU.not_equal, op1=ALU.max)\
                 .then_inc(recip_ready, 1)

            def take_o(t, d, c):
                dve.wait_ge(o_hi_ready, NC * t.batch(d) + (c + 1))
                v.tensor_tensor(o_lo[:, t.par(d), c, :], ps[:, PV_BANK, 0:N], o_hi[:, t.par(d), c, :],
                                ALU.subtract).then_inc(o_split, 1)

            def take_qk(t, j):
                dve.wait_ge(pj_hi, 4 * t.batch(1) + (j + 1))
                g = j % 2
                hi, lo = (q_hi, q_lo) if j < 2 else (k_hi, k_lo)
                v.scalar_tensor_tensor(out=lo[:, 2 * g:2 * g + 2, :].rearrange("p c n -> p (c n)"),
                                       in0=ps[:, PJ_BANK + g, :], scalar=-DOWN if j < 2 else DOWN,
                                       in1=hi[:, 2 * g:2 * g + 2, :].rearrange("p c n -> p (c n)"),
                                       op0=ALU.mult, op1=ALU.subtract).then_inc(pj_taken[g], taken_step(t, j))

            def check_adj(t):
                dve.wait_ge(adj_in[t.par(1)], 16 * t.half(1) + 16)
                v.tensor_reduce(out=adj_max[:, t.par(1), :], in_=adj_raw[:, t.par(1)], axis=AX.X, op=ALU.max,
                                apply_absolute_value=True).then_inc(adj_checked, 1)

            def test_rows(t):
                dve.wait_ge(aux_full, aux_at(t, 2))
                dve.wait_ge(adj_checked, t.batch(1) + 1)
                v.scalar_tensor_tensor(out=some_qk[:, t.par(1)],
                                       in0=ps[:, AUX_BANK, 0:NU * H].rearrange("p (u h) -> p u h", u=NU),
                                       scalar=0.0,
                                       in1=adj_max[:, t.par(1), :].unsqueeze(2).broadcast_to([P, NU, H]),
                                       op0=ALU.not_equal, op1=ALU.max).then_inc(rows_tested, 1)
                dve.wait_ge(rows_tested, 2 * t.batch(1) + 1)
                dve.sem_inc(aux_taken, 1)
                v.tensor_scalar(some_qk[:, t.par(1)], some_qk[:, t.par(1)], 0.0, None, ALU.not_equal)\
                 .then_inc(rows_tested, 1)

            def residual(t, u):
                dve.wait_ge(pj_full, pj_full_at(t, 4 + u))
                dve.wait_ge(xres_in[t.par(-1)], 16 * t.half(-1) + 16)
                v.scalar_tensor_tensor(out=x_res[:, t.par(-1), u, :], in0=ps[:, PJ_BANK + u, :],
                                       scalar=out_scale[:, 0:1], in1=x_res[:, t.par(-1), u, :],
                                       op0=ALU.mult, op1=ALU.add).then_inc(pj_taken[u], taken_step(t, 4 + u))

            def slot(t):
                for s in range(H):
                    take_probs_t(t, s - 1)
                    if t is second or t is last:
                        logit_rows(t, s + 2)
                        invert(t, s + 1)
                    else:
                        invert(t, s + 1)
                        logit_rows(t, s + 2)
                    if s == 2 and t.prev:
                        take_o(t, -1, NC - 1)
                    if s % 4 == 2 and s >= 4 and t.cur:
                        take_o(t, 0, s // 4 - 1)
                    if t.nxt:
                        if s == (5 if t.first else 0):
                            ln_sum(t, 2)
                        if s == (5 if t.first else 1):
                            ln_statistics(t, 2, 0)
                        if s == (5 if t.first else 3):
                            ln_statistics(t, 2, 1)
                            ln_mean_var(t, 2)
                        if s in (2, 4, 6, 8):
                            take_qk(t, s // 2 - 1)
                        if s == (9 if t.first else 5):
                            check_adj(t)
                        if s in take_h_steps(t):
                            k = take_h_steps(t).index(s)
                            take_h(t, 2, k, 2 * t.batch(2) + (k + 1))
                        if s == 13:
                            test_rows(t)
                    if t.prev and s in residual_steps(t):
                        residual(t, residual_steps(t).index(s))
                    if t.first:
                        if s == 3:
                            weight_max(2)
                        if s == 6:
                            weight_row_max(2)
                        if s == 7:
                            weight_scale(2)
                        if s == 8:
                            weight_rest(2)
                    if t is second:
                        if s == 2:
                            weight_max(3)
                        if s == 5:
                            weight_row_max(3)
                        if s == 6:
                            weight_scale(3)
                        if s - 1 in range(WO_STEP, WO_STEP + NC):
                            kc = s - 1 - WO_STEP
                            weight_chunk_rest(3, kc, PJ_BANK + kc % 2)

            run(dve, slot)

        @block.tensor
        def _(pe):
            mm, tr = nc.tensor.matmul, nc.tensor.transpose
            pe.wait_ge(ident_set, 1)

            def turn_h(t, d, k, n):
                pe.wait_ge(xn_ready, NU * (t.batch(d) + 1))
                need(pe, aux_taken, n - 1)
                for c in range(2):
                    for u in range(NU):
                        m = tr(ps[:, AUX_BANK, N * c + P * u:N * c + P * u + P],
                               xn[:, u, P * (2 * k + c):P * (2 * k + c) + P], ident[:])
                m.then_inc(aux_full, 1)

            def turn_weights(w, chunks=range(NC)):
                pe.wait_ge(w_in[w], 16)
                for kc in chunks:
                    n = NC * w + kc
                    need(pe, wt_taken, n - (W_BANKS - 1))
                    for o in range(NC):
                        m = tr(ps[:, n % W_BANKS, P * o:P * o + P], w_nat[:, w, o, P * kc:P * kc + P], ident[:])
                    m.then_inc(wt_ready, 1)

            def turn_max(w):
                pe.wait_ge(w_max_found, w + 1)
                need(pe, scale_step, 3 * w)
                if w == 3:
                    pe.wait_ge(aux_taken, aux_at(first, 2))
                tr(ps[0:1, max_bank(w), 0:P], w_max[:, w:w + 1], ident[:]).then_inc(w_row_turned, 1)

            def spread_max(w):
                pe.wait_ge(ones_set, 1)
                pe.wait_ge(w_row_max_found, w + 1)
                mm(ps[:, max_bank(w), TOP_COL + w:TOP_COL + w + 1], ones_row[:], w_row_max[0:1, w:w + 1],
                   start=True, stop=True).then_inc(w_top_found, 1)

            def turn_last_weights(kc):
                if kc < 2:
                    pe.wait_ge(pj_taken[kc], bank_free_at(second, 4 + kc))
                else:
                    pe.wait_ge(wt_taken, NC * 3 + kc - 1)
                for o in range(NC):
                    m = tr(ps[:, PJ_BANK + kc % 2, P * o:P * o + P], w_nat[:, 3, o, P * kc:P * kc + P], ident[:])
                m.then_inc(wt_ready, 1)

            turn_weights(0, (0, 1))
            turn_max(0)
            turn_h(first, 1, 0, 1)
            spread_max(0)
            turn_weights(0, (2, 3))
            turn_h(first, 1, 1, 2)
            turn_max(1)
            spread_max(1)
            turn_weights(1)

            THREE = ((0, 0), (0, 1), (1, 0))
            W = (w_hi, w_lo)
            HT = (ht_hi, ht_lo)
            O = (o_hi, o_lo)

            def part_products(t, j):
                out = []
                g = j % 2
                if j < 4:
                    w = j // 2
                    for c in range(2):
                        steps = [(kc, a, b) for kc in range(NC) for a, b in THREE]
                        for i, (kc, a, b) in enumerate(steps):
                            fs = P * (2 * g + c)
                            out.append((ps[:, PJ_BANK + g, N * c:N * c + N], W[a][:, w, kc, fs:fs + P],
                                        HT[b][:, t.par(1), kc, :], i == 0, i == len(steps) - 1))
                elif j < 6:
                    steps = [(c, a, b) for c in range(NC) for a, b in THREE]
                    for i, (c, a, b) in enumerate(steps):
                        out.append((ps[:, PJ_BANK + g, :], O[a][:, t.par(-1), c, P * g:P * g + P],
                                    W[b][:, 3, c, :], i == 0, i == len(steps) - 1))
                else:
                    steps = [(kc, a, b) for kc in range(NC) for a, b in THREE]
                    for i, (kc, a, b) in enumerate(steps):
                        out.append((ps[:, PJ_BANK + g, :], HT[a][:, t.par(1), kc, P * g:P * g + P],
                                    W[b][:, 2, kc, :], i == 0, i == len(steps) - 1))
                return out

            def project_last(t, d, c):
                pe.wait_ge(o_split, NC * t.batch(d) + (c + 1))
                for u in range(NU):
                    if c == 0:
                        pe.wait_ge(pj_taken[u], bank_free_at(tail, 4 + u))
                    for k, (a, b) in enumerate(THREE):
                        m = mm(ps[:, PJ_BANK + u, :], O[a][:, t.par(d), c, P * u:P * u + P], W[b][:, 3, c, :],
                               start=(c == 0 and k == 0), stop=(c == NC - 1 and k == len(THREE) - 1))
                    if c == NC - 1:
                        m.then_inc(pj_full, full_step(tail, 4 + u))

            def project(t, s):
                j, part = s // 2, s % 2
                if not t.uses(j) or t is tail:
                    return
                if part == 0:
                    need(pe, pj_taken[j % 2], bank_free_at(t, j))
                    if j == 0:
                        pe.wait_ge(aux_taken, 2 if t.first else aux_at(t, 1) - 3)
                    if j == 4:
                        pe.wait_ge(o_split, NC * t.batch(0))
                    if t.first and j in (0, 2, 6):
                        pe.wait_ge(wt_taken, NC * (1 + {0: 0, 2: 1, 6: 2}[j]))
                    if t is second and j in (6, 7):
                        pe.wait_ge(wt_taken, NC * 3 + NC - 7 + j)
                products = part_products(t, j)
                half = len(products) // 2
                for o, l, r, start, stop in products[half * part:half * part + half]:
                    m = mm(o, l, r, start=start, stop=stop)
                if part == 1:
                    m.then_inc(pj_full, full_step(t, j))

            def scores(t, s):
                d, h = head(t, s)
                if d is None:
                    return
                c, j = h // HC, h % HC
                if h == 0:
                    pe.wait_ge(q_stacked, 16 * NK * HC * (t.batch(d) + 1))
                if h < HC:
                    pe.wait_ge(k_stacked[j], 16 * NK * (t.batch(d) + 1))
                need(pe, logits_ready, NU * (H * t.batch(d) + (h - 1)))
                for u in range(NU):
                    m = mm(ps[:, S_BANK + h % 2, N * u:N * u + N], q_stack[:, t.par(d), j, c, P * u:P * u + P],
                           k_stack[:, t.par(d), j, c, :], start=True, stop=True)
                m.then_inc(scores_ready, 1)

            def turn_probs(t, s):
                d, h = head(t, s)
                if d is None:
                    return
                pe.wait_ge(probs_scaled, H * t.batch(d) + (h + 1))
                need(pe, pt_taken[h % 2], (H // 2) * t.batch(d) + h // 2)
                for mh in range(NU):
                    for u in range(NU):
                        m = tr(ps[:, PT_BANK + h % 2, N * mh + P * u:N * mh + P * u + P],
                               probs[:, h % 4, u, P * mh:P * mh + P], ident[:])
                m.then_inc(pt_full, 1)

            def values(t, d, c):
                for i in range(2):
                    pe.wait_ge(pt_taken[i], (H // 2) * t.batch(d) + 2 * (c + 1))
                need(pe, o_split, NC * t.batch(d) + c)
                if t is second and c == 0:
                    pe.wait_ge(scale_step, 3 * 2 + 1)
                if c == 0:
                    for u in range(NU):
                        pe.wait_ge(pj_taken[u], (NJ // 2) * (t.batch(d) + 1))
                for mh in range(NU):
                    for j in range(HC):
                        h = HC * c + j
                        m = mm(ps[HD * j:HD * j + HD, PV_BANK, 0:N],
                               v_sb[:, t.par(d), mh, HD * h:HD * h + HD], probs_t[:, h % 8, mh, :],
                               start=(mh == 0), stop=(mh == NU - 1))
                m.then_inc(pv_done, 1)

            def row_test(t):
                pe.wait_ge(k_diag_ready, t.batch(1) + 1)
                pe.wait_ge(aux_taken, aux_at(t, 2) - 1)
                for u in range(NU):
                    for c in range(NC):
                        m = mm(ps[:, AUX_BANK, H * u + HC * c:H * u + HC * c + HC],
                               q_hi[:, c, P * u:P * u + P], k_diag[:, c, :], start=True, stop=True)
                m.then_inc(aux_full, 1)

            def slot(t):
                for s in range(H):
                    if t.first:
                        if s == 7:
                            turn_max(2)
                        if s == 8:
                            spread_max(2)
                            turn_weights(2)
                    if t is second:
                        if s == 4:
                            turn_max(3)
                        if s == 6:
                            spread_max(3)
                        if s == 7:
                            pe.wait_ge(scale_step, 3 * 3 + 1)
                    if t.first and s == H - 2:
                        pe.wait_ge(wt_taken, 3 * NC)
                    if not t.first:
                        scores(t, s + 3)
                    elif s == H - 2:
                        scores(t, H)
                        scores(t, H + 1)
                    elif s == H - 1:
                        scores(t, H + 2)
                    if t is not last:
                        project(t, s)
                    elif s in (4, 5, 6, 7):
                        project(t, s + 4)
                    turn_probs(t, s)
                    if t.nxt:
                        if s in turn_h_steps(t):
                            k = turn_h_steps(t).index(s)
                            turn_h(t, 2, k, aux_at(t, k))
                        if s == (13 if t.first else 12):
                            row_test(t)
                    if s == 0 and t.prev:
                        values(t, -1, NC - 1)
                    if t.cur and s >= 4 and s % 4 == 0:
                        values(t, 0, s // 4 - 1)
                    if t is second and s in range(WO_STEP, WO_STEP + NC):
                        turn_last_weights(s - WO_STEP)
                    if t is last and s in (9, 13):
                        project_last(t, 0, s // 13)
                    if t is tail and s in (1, 2):
                        project_last(t, -1, NC - 3 + s)

            run(pe, slot)


_INS = ["x", "adj", "L0_gnn_Wq", "L0_gnn_Wk", "L0_gnn_Wv", "L0_gnn_Wo"]


def kernel(**inputs):
    import numpy as _np
    import concourse.bacc as _bacc
    from concourse import mybir as _mybir
    from concourse.bass_utils import run_bass_kernel_spmd as _run

    nc = _bacc.Bacc("TRN2", target_bir_lowering=False, num_devices=1)
    arrays, args = {}, []
    for name in _INS:
        a = _np.ascontiguousarray(inputs[name])
        arrays[f"in_{name}"] = a
        args.append(nc.dram_tensor(f"in_{name}", a.shape, _mybir.dt.from_np(a.dtype), kind="ExternalInput").ap())
    out = nc.dram_tensor("out_0", inputs["x"].shape, _mybir.dt.float32, kind="ExternalOutput").ap()
    emit(nc, *args, out)
    return _run(nc, [arrays], core_ids=[0]).results[0]["out_0"]
```
